# Optimizing a Trainium2 kernel written in Bass

```python
import numpy as np
import jax
import jax.numpy as jnp

def _softmax(x, axis=-1):
    return jax.nn.softmax(x, axis=axis)

def _gelu(x):
    return jax.nn.gelu(x, approximate=True)

def _silu(x):
    return jax.nn.silu(x)

def _sigmoid(x):
    return jax.nn.sigmoid(x)

def _layernorm(x, axis=-1, eps=1e-05):
    m = jnp.mean(x, axis=axis, keepdims=True)
    v = jnp.var(x, axis=axis, keepdims=True)
    return (x - m) / jnp.sqrt(v + eps)

def _scatter_add(tgt, idx, src, axis=0):
    return tgt.at[idx].add(src)

def _segment_sum(src, seg, n):
    return jax.ops.segment_sum(src, seg, n)
kernel_name = 'mk_cond_seq_d2_seqx_r4_d7d582'

def setup_inputs(seed: int=0):
    np.random.seed(seed)
    _w = jnp.asarray

    def _rec_inputs():
        import jax
        import jax.numpy as jnp
        _rk = jax.random.key(seed)
        x = -0.0002928 + 1 * jax.random.normal(jax.random.fold_in(_rk, 1), (2, 1024, 256), jnp.float32)
        _lenS = 1024 - jax.random.randint(jax.random.fold_in(_rk, 7), (2,), 0, max(1, 1024 // 4) + 1, jnp.int32)
        _lenS2 = 1024 - jax.random.randint(jax.random.fold_in(_rk, 8), (2,), 0, max(1, 1024 // 4) + 1, jnp.int32)
        cond_1024 = 0.0061147 + 1.02565 * jax.random.normal(jax.random.fold_in(_rk, 11), (2, 256), jnp.float32)
        return (x, cond_1024)
    x, cond_1024 = _rec_inputs()

    def _L0_cond_setup():
        import jax, jax.numpy as jnp
        import numpy as np
        B, T, DIM = (4, 256, 256)
        COND = 256
        HEADS, DH = (16, 64)
        INNER = HEADS * DH
        MLP = 1024
        EPS = 1e-05

        def _layernorm(x):
            mu = jnp.mean(x, axis=-1, keepdims=True)
            var = jnp.mean(jnp.square(x - mu), axis=-1, keepdims=True)
            return (x - mu) * jax.lax.rsqrt(var + EPS)

        def _modulate(x, shift, scale):
            return x * (1.0 + scale) + shift

        def _attention(x, W_qkv, W_out, b_out):
            Bq, Tq, _ = x.shape
            qkv = x @ W_qkv
            q, k, v = jnp.split(qkv, 3, axis=-1)
            q = q.reshape(Bq, Tq, HEADS, DH)
            k = k.reshape(Bq, Tq, HEADS, DH)
            v = v.reshape(Bq, Tq, HEADS, DH)
            scale = DH ** (-0.5)
            attn = jnp.einsum('bqhd,bkhd->bhqk', q, k) * scale
            attn = jax.nn.softmax(attn, axis=-1)
            out = jnp.einsum('bhqk,bkhd->bqhd', attn, v).reshape(Bq, Tq, INNER)
            return out @ W_out + b_out

        def _ff(x, W1, b1, W2, b2):
            return jax.nn.gelu(x @ W1 + b1, approximate=False) @ W2 + b2
        key = jax.random.key(seed)
        ks = jax.random.split(key, 12)
        s = 0.02
        return {'x': jax.random.normal(ks[0], (B, T, DIM), jnp.float32), 'c': jax.random.normal(ks[1], (B, 1, COND), jnp.float32), 'W_mod': jax.random.normal(ks[2], (COND, 6 * DIM), jnp.float32) * s, 'b_mod': jax.random.normal(ks[3], (6 * DIM,), jnp.float32) * s, 'W_qkv': jax.random.normal(ks[4], (DIM, 3 * INNER), jnp.float32) * s, 'W_out': jax.random.normal(ks[5], (INNER, DIM), jnp.float32) * s, 'b_out': jax.random.normal(ks[6], (DIM,), jnp.float32) * s, 'W1': jax.random.normal(ks[7], (DIM, MLP), jnp.float32) * s, 'b1': jax.random.normal(ks[8], (MLP,), jnp.float32) * s, 'W2': jax.random.normal(ks[9], (MLP, DIM), jnp.float32) * s, 'b2': jax.random.normal(ks[10], (DIM,), jnp.float32) * s}
    _L0_cond_all = _L0_cond_setup()
    _L0_cond_in = {k: v for k, v in _L0_cond_all.items() if k in ('W_mod', 'b_mod', 'W_qkv', 'W_out', 'b_out', 'W1', 'b1', 'W2', 'b2')}
    del _L0_cond_all

    def _L1_cond_setup():
        import jax, jax.numpy as jnp
        import numpy as np
        H = 16
        EPS = 1e-05

        def layer_norm(x, g, b):
            mu = jnp.mean(x, axis=-1, keepdims=True)
            var = jnp.var(x, axis=-1, keepdims=True)
            return (x - mu) * jax.lax.rsqrt(var + EPS) * g + b
        key = jax.random.key(seed)
        ks = jax.random.split(key, 8)
        B, T, D, TE = (4, 1024, 256, 256)
        s = 0.02
        return {'x': jax.random.normal(ks[0], (B, T, D), jnp.float32), 'emb': jax.random.normal(ks[1], (B, 1, TE), jnp.float32), 'gate_msa': jax.random.normal(ks[2], (B, 1, D), jnp.float32), 'norm_g': jnp.ones((D,), jnp.float32), 'norm_b': jnp.zeros((D,), jnp.float32), 'Wq': jax.random.normal(ks[3], (D, D), jnp.float32) * s, 'bq': jnp.zeros((D,), jnp.float32), 'Wk': jax.random.normal(ks[4], (D, D), jnp.float32) * s, 'bk': jnp.zeros((D,), jnp.float32), 'Wv': jax.random.normal(ks[5], (D, D), jnp.float32) * s, 'bv': jnp.zeros((D,), jnp.float32), 'emb_W': jax.random.normal(ks[6], (TE, 2 * D), jnp.float32) * s, 'emb_b': jnp.zeros((2 * D,), jnp.float32), 'sn_g': jnp.ones((D,), jnp.float32), 'sn_b': jnp.zeros((D,), jnp.float32), 'out_W': jax.random.normal(ks[7], (D, D), jnp.float32) * s, 'out_b': jnp.zeros((D,), jnp.float32)}
    _L1_cond_all = _L1_cond_setup()
    _L1_cond_in = {k: v for k, v in _L1_cond_all.items() if k in ('norm_g', 'norm_b', 'Wq', 'bq', 'Wk', 'bk', 'Wv', 'bv', 'emb_W', 'emb_b', 'sn_g', 'sn_b', 'out_W', 'out_b')}
    del _L1_cond_all
    return {'x': x, 'cond_1024': cond_1024, 'L0_cond_W_mod': _L0_cond_in['W_mod'], 'L0_cond_b_mod': _L0_cond_in['b_mod'], 'L0_cond_W_qkv': _L0_cond_in['W_qkv'], 'L0_cond_W_out': _L0_cond_in['W_out'], 'L0_cond_b_out': _L0_cond_in['b_out'], 'L0_cond_W1': _L0_cond_in['W1'], 'L0_cond_b1': _L0_cond_in['b1'], 'L0_cond_W2': _L0_cond_in['W2'], 'L0_cond_b2': _L0_cond_in['b2'], 'L1_cond_norm_g': _L1_cond_in['norm_g'], 'L1_cond_norm_b': _L1_cond_in['norm_b'], 'L1_cond_Wq': _L1_cond_in['Wq'], 'L1_cond_bq': _L1_cond_in['bq'], 'L1_cond_Wk': _L1_cond_in['Wk'], 'L1_cond_bk': _L1_cond_in['bk'], 'L1_cond_Wv': _L1_cond_in['Wv'], 'L1_cond_bv': _L1_cond_in['bv'], 'L1_cond_emb_W': _L1_cond_in['emb_W'], 'L1_cond_emb_b': _L1_cond_in['emb_b'], 'L1_cond_sn_g': _L1_cond_in['sn_g'], 'L1_cond_sn_b': _L1_cond_in['sn_b'], 'L1_cond_out_W': _L1_cond_in['out_W'], 'L1_cond_out_b': _L1_cond_in['out_b']}

def reference(x, cond_1024, L0_cond_W_mod, L0_cond_b_mod, L0_cond_W_qkv, L0_cond_W_out, L0_cond_b_out, L0_cond_W1, L0_cond_b1, L0_cond_W2, L0_cond_b2, L1_cond_norm_g, L1_cond_norm_b, L1_cond_Wq, L1_cond_bq, L1_cond_Wk, L1_cond_bk, L1_cond_Wv, L1_cond_bv, L1_cond_emb_W, L1_cond_emb_b, L1_cond_sn_g, L1_cond_sn_b, L1_cond_out_W, L1_cond_out_b):
    import jax
    import jax.numpy as jnp

    def _L0_cond_ref(x, c, W_mod, b_mod, W_qkv, W_out, b_out, W1, b1, W2, b2):
        import jax, jax.numpy as jnp
        import numpy as np
        B, T, DIM = (4, 256, 256)
        COND = 256
        HEADS, DH = (16, 64)
        INNER = HEADS * DH
        MLP = 1024
        EPS = 1e-05

        def _layernorm(x):
            mu = jnp.mean(x, axis=-1, keepdims=True)
            var = jnp.mean(jnp.square(x - mu), axis=-1, keepdims=True)
            return (x - mu) * jax.lax.rsqrt(var + EPS)

        def _modulate(x, shift, scale):
            return x * (1.0 + scale) + shift

        def _attention(x, W_qkv, W_out, b_out):
            Bq, Tq, _ = x.shape
            qkv = x @ W_qkv
            q, k, v = jnp.split(qkv, 3, axis=-1)
            q = q.reshape(Bq, Tq, HEADS, DH)
            k = k.reshape(Bq, Tq, HEADS, DH)
            v = v.reshape(Bq, Tq, HEADS, DH)
            scale = DH ** (-0.5)
            attn = jnp.einsum('bqhd,bkhd->bhqk', q, k) * scale
            attn = jax.nn.softmax(attn, axis=-1)
            out = jnp.einsum('bhqk,bkhd->bqhd', attn, v).reshape(Bq, Tq, INNER)
            return out @ W_out + b_out

        def _ff(x, W1, b1, W2, b2):
            return jax.nn.gelu(x @ W1 + b1, approximate=False) @ W2 + b2
        mod = jax.nn.silu(c) @ W_mod + b_mod
        sh_msa, sc_msa, g_msa, sh_mlp, sc_mlp, g_mlp = jnp.split(mod, 6, axis=-1)
        x = x + g_msa * _attention(_modulate(_layernorm(x), sh_msa, sc_msa), W_qkv, W_out, b_out)
        x = x + g_mlp * _ff(_modulate(_layernorm(x), sh_mlp, sc_mlp), W1, b1, W2, b2)
        return x

    def _L1_cond_ref(x, emb, gate_msa, norm_g, norm_b, Wq, bq, Wk, bk, Wv, bv, emb_W, emb_b, sn_g, sn_b, out_W, out_b):
        import jax, jax.numpy as jnp
        import numpy as np
        H = 16
        EPS = 1e-05

        def layer_norm(x, g, b):
            mu = jnp.mean(x, axis=-1, keepdims=True)
            var = jnp.var(x, axis=-1, keepdims=True)
            return (x - mu) * jax.lax.rsqrt(var + EPS) * g + b
        B, T, D = x.shape
        dh = D // H
        xn = layer_norm(x, norm_g, norm_b)
        q = (xn @ Wq + bq).reshape(B, T, H, dh)
        k = (xn @ Wk + bk).reshape(B, T, H, dh)
        v = (xn @ Wv + bv).reshape(B, T, H, dh)
        q = jax.nn.softmax(q, axis=-1)
        k = jax.nn.softmax(k, axis=1)
        ctx = jnp.einsum('bnhd,bnhl->bhdl', k, v)
        y = jnp.einsum('bnhd,bhdl->bnhl', q, ctx).reshape(B, T, D)
        emb_out = jax.nn.silu(emb) @ emb_W + emb_b
        scale, shift = jnp.split(emb_out, 2, axis=-1)
        h = layer_norm(y, sn_g, sn_b) * (1.0 + scale) + shift
        h = jax.nn.silu(h) @ out_W + out_b
        return x + gate_msa * h
    x = _L0_cond_ref(x, cond_1024[:, None, :], L0_cond_W_mod, L0_cond_b_mod, L0_cond_W_qkv, L0_cond_W_out, L0_cond_b_out, L0_cond_W1, L0_cond_b1, L0_cond_W2, L0_cond_b2)
    x = _L1_cond_ref(x, cond_1024[:, None, :], cond_1024[:, None, :], L1_cond_norm_g, L1_cond_norm_b, L1_cond_Wq, L1_cond_bq, L1_cond_Wk, L1_cond_bk, L1_cond_Wv, L1_cond_bv, L1_cond_emb_W, L1_cond_emb_b, L1_cond_sn_g, L1_cond_sn_b, L1_cond_out_W, L1_cond_out_b)
    return x

_drawn_inputs = setup_inputs


def setup_inputs(seed=0):
    import zlib

    import numpy as np

    out = dict(_drawn_inputs(seed))
    spreads = {'L1_cond_norm_g': (1.0, 0.6),
     'L1_cond_norm_b': (0.0, 0.319),
     'L1_cond_bq': (0.0, 0.8),
     'L1_cond_bk': (0.0, 2.0),
     'L1_cond_bv': (0.0, 0.1),
     'L1_cond_emb_b': (0.0, 0.275),
     'L1_cond_sn_g': (1.0, 0.2),
     'L1_cond_sn_b': (0.0, 0.42),
     'L1_cond_out_b': (0.0, 0.1)}
    factors = {'L0_cond_b_mod': 8.0,
     'L0_cond_W_qkv': 5.275,
     'L0_cond_W_out': 4.896,
     'L0_cond_b_out': 8.0,
     'L0_cond_b1': 36.024,
     'L0_cond_b2': 8.0,
     'L1_cond_Wq': 8.0,
     'L1_cond_Wk': 8.0}
    for name, (base, spread) in spreads.items():
        noise = np.random.default_rng([zlib.crc32(name.encode()), seed]).standard_normal(out[name].shape)
        drawn = base * np.exp(spread * noise) if base else spread * noise
        out[name] = jnp.asarray(drawn.astype(out[name].dtype))
    for name, factor in factors.items():
        out[name] = (out[name] * factor).astype(out[name].dtype)
    return out
```

```python
from contextlib import ExitStack

import concourse.bass as bass
from concourse import mybir

F32 = mybir.dt.float32
F32R = mybir.dt.float32r
ACT = mybir.ActivationFunctionType
ALU = mybir.AluOpType
AX = mybir.AxisListType

P = 128
B, T, D = 2, 1024, 256
KD = D // P
TT = T // P
CH = 512
NC = T // CH
TPC = CH // P
HEADS, DH = 16, 64
PAIRS = HEADS // 2
MLP = 1024
MB = MLP // P
H1, DH1 = 16, 16
EPS = 1e-5
STEPS = NC * TT

ST_CREDIT = STEPS + 1
EXP_CREDIT = 2
PV_CREDIT = STEPS + 4
PRESUM_CREDIT = TT - 1
SUM_CREDIT = 2
DMA_CREDIT = 16

RING_PRO = 6 + 2 + 16
RING_IT = 16 + RING_PRO
RING_B = RING_PRO + (PAIRS - 1) * RING_IT + 16
SMALL_B = 4 * PAIRS

SIDE = {
    0: [("max", 1, 0), ("max", 1, 1)],
    1: [("sum", 1), ("max", 1, 2), ("max", 1, 3)],
    2: [("max", 1, 4), ("max", 1, 5), ("proj", 0)],
    3: [("max", 1, 6), ("max", 1, 7), ("proj", 1)],
    4: [("m", 1), ("proj", 2), ("proj", 3)],
    5: [("proj", 4)],
    6: [("proj", 5)],
    7: [("vt", 0)],
    8: [("vt", 1)],
    9: [("sum", 0)],
    10: [("max", 0, 0), ("max", 0, 1)],
    11: [("max", 0, 2), ("max", 0, 3)],
    12: [("max", 0, 4), ("max", 0, 5)],
    13: [("max", 0, 6), ("max", 0, 7)],
    14: [("m", 0)],
    15: [],
}
PROLOGUE = [("proj", k) for k in range(6)] + [("vt", 0), ("vt", 1)] \
    + [("max", 0, u) for u in range(8)] + [("m", 0)]


def side_items(p, s):
    out = []
    for item in SIDE[s]:
        of_next = item[0] in ("proj", "vt") or item[0] in ("max", "m") and item[1] == 0
        if of_next and isinstance(p, int) and p == PAIRS - 1:
            continue
        if item == ("sum", 1) and isinstance(p, int) and p == 0:
            continue
        out.append((of_next,) + item)
    return out


def wait_alone(eng, sem, value, tick):
    eng.wait_ge(sem, value)
    eng.sem_inc(tick, 1)


class Ring:

    def __init__(self, base):
        self.base, self.k = base, 0

    def take(self):
        bank, before = self.k % 2, self.base + self.k // 2
        self.k += 1
        return bank, before


def for_pairs(eng, emit):
    emit(0, 0)
    with eng.Fori(0, (PAIRS - 2) // 2) as two:
        emit(two * 2 + 1, 1)
        emit(two * 2 + 2, 0)
    emit(PAIRS - 1, 1)


def dit_kernel(nc, x, cond, W_mod, b_mod, W_qkv, W_out, b_out, W1, b1, W2, b2,
               norm_g, norm_b, Wq, bq, Wk, bk, Wv, bv, emb_W, emb_b, sn_g, sn_b, out_W, out_b, out):
    with ExitStack() as ctx:
        place = [(nc.sbuf_base + 31) // 32 * 32]

        def at(name, shape, dt, offset):
            return nc.alloc_sbuf_tensor_at(name, shape, dt, offset=offset)

        def sb(name, shape, dt=F32):
            n = 4
            for s in shape[1:]:
                n *= s
            t = at(name, shape, dt, place[0])
            place[0] += (n + 31) // 32 * 32
            return t

        def sem(name):
            return ctx.enter_context(nc.semaphore(name))

        ident = sb("ident", [P, P])
        ones = sb("ones", [P, DH])
        blockdiag = sb("blockdiag", [P, P])
        gates = sb("gates", [P, B, 3, D])
        rowbias = sb("rowbias", [P, 3, D])
        affs = sb("affs", [P, B, 2, 4, KD])
        aff = sb("aff", [P, 2, 4, KD])
        b1c = sb("b1c", [P, MB])
        bkc = sb("bkc", [P, KD])
        nhalf = sb("nhalf", [P, TPC])
        small = sb("small", [P, 64])
        ktmp, knb, ksum, krs = small[:, 0:2], small[:, 2:4], small[:, 4:6], small[:, 6:8]
        kmx = small[:, 8:10]
        stat = sb("stat", [P, TT, 6])
        mv = sb("mv", [P, TT, 2])
        veps = sb("veps", [P, TT])
        rstd = sb("rstd", [P, TT])
        xs = sb("xs", [P, TT, D])
        xnh = sb("xnh", [P, KD, T], F32R)
        xnl = sb("xnl", [P, KD, T], F32R)
        OT = sb("OT", [P, PAIRS, T])
        Wo = sb("Wo", [P, PAIRS, D])
        wraw = sb("wraw", [P, KD, 3, P])
        wh = sb("wh", [P, KD, 3, P], F32R)
        wl = sb("wl", [P, KD, 3, P], F32R)
        vn = [sb(f"vn{i}", [P, TT, P]) for i in range(2)]
        vT0 = place[0]
        vT = sb("vT", [P, T])
        cm = at("cm", [P, KD, P], F32, vT0)
        qmx = at("qmx", [P, TT, H1], F32, vT0 + 1024)
        qsum = at("qsum", [P, TT, H1], F32, vT0 + 1536)
        qrs = at("qrs", [P, TT, H1], F32, vT0 + 2048)
        acc = sb("acc", [P, NC, 2, CH])
        rtmp = at("rtmp", [P, 2, D], F32, place[0])
        o_raw = sb("o_raw", [P, CH])
        rec = sb("rec", [P, CH])
        mpart = sb("mpart", [P, 8, 2])
        mx = sb("mx", [P, 8])
        ml = sb("ml", [P, TPC, 2, 2], F32R)
        mrow = sb("mrow", [4, CH], F32R)
        pb0 = place[0]
        pb = sb("pb", [P, 4, 2, CH])
        xh = at("xh", [P, TT, D], F32, pb0)
        xT = at("xT", [P, KD, T], F32, pb0 + 8192)
        sg0 = place[0]
        qh = sb("qh", [P, T], F32R)
        ql = sb("ql", [P, T], F32R)
        kh = sb("kh", [P, T], F32R)
        kl = sb("kl", [P, T], F32R)
        Wqv = at("Wqv", [P, KD, 2 * D], F32, sg0)
        Wks = at("Wks", [P, KD, D], F32, sg0 + 4096)
        oW = at("oW", [P, KD, D], F32, sg0 + 6144)
        qvbias = at("qvbias", [P, 2 * D], F32, sg0 + 8192)
        k0 = place[0]
        qq = [[sb(f"qq{i}{h}", [P, T], F32R) for h in range(2)] for i in range(2)]
        kk = [[sb(f"kk{i}{h}", [P, T], F32R) for h in range(2)] for i in range(2)]
        qm = [[sb(f"qm{i}{h}", [P, T], F32R) for h in range(2)] for i in range(2)]
        km = [[sb(f"km{i}{h}", [P, T], F32R) for h in range(2)] for i in range(2)]
        assert place[0] <= nc.sbuf_usable_end, place[0]
        W1s = at("W1s", [P, KD, MLP], F32, k0)
        W2s = at("W2s", [P, MB, D], F32, k0 + 8192)
        KE = at("KE", [P, KD, T], F32, k0 + 16384)
        KN = at("KN", [P, TT, D], F32, k0 + 24576)
        QV = at("QV", [P, TT, 2 * D], F32, k0 + 32768)
        QT = at("QT", [P, KD, T], F32, k0 + 49152)
        Y = at("Y", [P, TT, D], F32, k0 + 57344)
        Wm = at("Wm", [P, KD, 6 * D], F32, k0)
        We = at("We", [P, KD, 2 * D], F32, k0 + 12288)
        cT = at("cT", [P, B, KD], F32, k0 + 16384)
        sc = at("sc", [P, B, KD], F32, k0 + 16384 + 32)
        cols = at("cols", [P, 16], F32, k0 + 16384 + 64)
        mc = at("mc", [P, 16, B], F32, k0 + 16384 + 128)
        lnp = at("lnp", [P, 4, KD], F32, k0 + 16384 + 256)
        gb = at("gb", [P, 2, D], F32, k0 + 16384 + 512)
        scb = at("scb", [P, B, KD, P], F32, k0 + 16384 + 4096)

        ps = ctx.enter_context(nc.psum_tensor("ps", [P, 8, 512], F32))
        st = [ps[:, 0:2, :], ps[:, 2:4, :]]
        o_ps = ps[:, 4, :]
        small_ps = ps[:, 5, :]
        ring = [ps[:, 6, :], ps[:, 7, :]]
        y_ps = [ps[:, 4, 0:D], ps[:, 5, 0:D]]

        const_ld = sem("const_ld")
        tick = sem("tick")
        wo_ld = sem("wo_ld")
        mask_a, mask_b, consts = sem("mask_a"), sem("mask_b"), sem("consts")
        silu_done, scb_done, modps, mod_done, mod_step = (sem("silu_done"), sem("scb_done"), sem("modps"), sem("mod_done"), sem("mod_step"))
        aff_done = sem("aff_done")
        x_ld, x_st = sem("x_ld"), sem("x_st")
        stat_done, mv_done, veps_done, rstd_done, xhat_done = (
            sem("stat_done"), sem("mv_done"), sem("veps_done"), sem("rstd_done"), sem("xhat_done"))
        lnT_full, lnT_done, xnh_done, xnl_done = sem("lnT_full"), sem("lnT_done"), sem("xnh_done"), sem("xnl_done")
        w_ld, wh_done, w_done, neg_done = sem("w_ld"), sem("wh_done"), sem("w_done"), sem("neg_done")
        ring_full = [sem("ring_full0"), sem("ring_full1")]
        ring_free = [sem("ring_free0"), sem("ring_free1")]
        small_free, mT_full, sum_full = sem("small_free"), sem("mT_full"), sem("sum_full")
        lead_done, rest_done, vT_done, asm_ld = sem("lead_done"), sem("rest_done"), sem("vT_done"), sem("asm_ld")
        mx_step, m_ld = sem("mx_step"), sem("m_ld")
        st_full, exp_done, pv_done, presum_done = sem("st_full"), sem("exp_done"), sem("pv_done"), sem("presum_done")
        o_free, norm_done = sem("o_free"), sem("norm_done")
        y_full, y_free, r_step, resid_done = sem("y_full"), sem("y_free"), sem("r_step"), sem("resid_done")
        post_ld = [sem("w1_ld"), sem("w2_ld"), sem("l1_ld")]
        h_full, gelu_done = sem("h_full"), sem("gelu_done")
        kt_full, kb_step, ke_done, krs_done, kn_full, kn_done = (
            sem("kt_full"), sem("kb_step"), sem("ke_done"), sem("krs_done"), sem("kn_full"), sem("kn_done"))
        qv_full, qv_done, qsub_done, qexp_done, q_step, q_done = (
            sem("qv_full"), sem("qv_done"), sem("qsub_done"), sem("qexp_done"), sem("q_step"), sem("q_done"))
        qt_full, qt_done, ctx_full, ctx_done, ya_full, ya_done = (
            sem("qt_full"), sem("qt_done"), sem("ctx_full"), sem("ctx_done"), sem("ya_full"), sem("ya_done"))

        x_v = x.rearrange("b (t p) d -> b p t d", p=P)
        out_v = out.rearrange("b (t p) d -> b p t d", p=P)
        rows = "(k p) n -> p k n"
        wqkv_v = W_qkv.rearrange("(k p) (s n) -> k p s n", p=P, s=3)

        block = ctx.enter_context(nc.Block())

        @block.sync
        def _(sp):
            N_CONST = [0]

            def const(dst, src):
                sp.dma_start(dst, src).then_inc(const_ld, 16)
                N_CONST[0] += 1

            with nc.allow_non_contiguous_dma(reason="small vectors into columns"):
                const(cT[:, :, :], cond.rearrange("b (k p) -> p b k", p=P))
                const(cols[:, 0:12], b_mod.rearrange("(j p) -> p j", p=P))
                const(cols[:, 12:16], emb_b.rearrange("(j p) -> p j", p=P))
                for n, v in enumerate((norm_g, norm_b, sn_g, sn_b)):
                    const(lnp[:, n, :], v.rearrange("(j p) -> p j", p=P))
                const(b1c[:, :], b1.rearrange("(j p) -> p j", p=P))
                const(bkc[:, :], bk.rearrange("(j p) -> p j", p=P))
                const(Wm[:, :, :], W_mod.rearrange(rows, p=P))
                const(We[:, :, :], emb_W.rearrange(rows, p=P))
                const(gb[:, 0, :], b_mod[2 * D:3 * D].partition_broadcast(P))
                const(gb[:, 1, :], b_mod[5 * D:6 * D].partition_broadcast(P))
                for b in range(B):
                    const(gates[:, b, 2, :], cond[b, :].partition_broadcast(P))
                for n, v in enumerate((b_out, b2, out_b)):
                    const(rowbias[:, n, :], v.partition_broadcast(P))
            assert N_CONST[0] == N_CONST_DMAS
            sp.dma_start(Wo[:, :, :], W_out.rearrange(rows, p=P)).then_inc(wo_ld, 16)

            def load_w(b, p):
                g = b * PAIRS + p
                sp.wait_ge(w_done, g + 1)
                for k in range(KD):
                    sp.dma_start(wraw[:, k, :, :], wqkv_v[k, :, :, bass.ds(p * P, P)]).then_inc(w_ld, 16)

            def assemble(b, p, par, k):
                g = b * PAIRS + p
                cs = slice((k // 2) * CH, (k // 2 + 1) * CH)
                if k == 0:
                    sp.wait_ge(st_full, g * STEPS + ST_CREDIT - STEPS)
                sp.wait_ge(rest_done, g * 4 + k + 1)
                for h in range(2):
                    s = slice(h * DH, (h + 1) * DH)
                    if k % 2 == 0:
                        moves = [(qq[par][h][0:DH, cs], qh[s, cs]), (qm[par][h][0:DH, cs], qh[s, cs]),
                                 (qq[par][h][DH:P, cs], ql[s, cs])]
                    else:
                        moves = [(kk[par][h][0:DH, cs], kh[s, cs]), (kk[par][h][DH:P, cs], kh[s, cs]),
                                 (km[par][h][0:DH, cs], kl[s, cs])]
                    for dst, src in moves:
                        sp.dma_start(dst.bitcast(F32), src.bitcast(F32)).then_inc(asm_ld, 16)

            def max_rows(b, p, par, c, used):
                sp.wait_ge(small_free, b * SMALL_B + used + 2)
                for h in range(2):
                    sp.dma_start(qm[par][h][DH:DH + 2, c * CH:(c + 1) * CH].bitcast(F32),
                                 mrow[2 * h:2 * h + 2, :].bitcast(F32)).then_inc(m_ld, 16)

            with sp.Fori(0, B) as b:
                sp.wait_ge(x_st, b * 32 + DMA_CREDIT)
                for h in range(2):
                    sp.dma_start(xs[:, h * 4:h * 4 + 4, :], x_v[b, :, h * 4:h * 4 + 4, :]).then_inc(x_ld, 16)
                load_w(b, 0)
                for k in range(4):
                    assemble(b, 0, 0, k)
                max_rows(b, 0, 0, 0, 0)

                def pair(p, par):
                    last = isinstance(p, int) and p == PAIRS - 1
                    if not last:
                        load_w(b, p + 1)
                        assemble(b, p + 1, 1 - par, 0)
                        assemble(b, p + 1, 1 - par, 1)
                    max_rows(b, p, par, 1, p * 4 + 1)
                    if not last:
                        assemble(b, p + 1, 1 - par, 2)
                        assemble(b, p + 1, 1 - par, 3)
                        max_rows(b, p + 1, 1 - par, 0, p * 4 + 3)

                for_pairs(sp, pair)
                sp.wait_ge(st_full, (b + 1) * PAIRS * STEPS + ST_CREDIT)
                sp.dma_start(W1s[:, :, :], W1.rearrange(rows, p=P)).then_inc(post_ld[0], 16)
                sp.dma_start(W2s[:, :, :], W2.rearrange(rows, p=P)).then_inc(post_ld[1], 16)
                sp.dma_start(Wqv[:, :, 0:D], Wq.rearrange(rows, p=P)).then_inc(post_ld[2], 16)
                sp.dma_start(Wqv[:, :, D:2 * D], Wv.rearrange(rows, p=P)).then_inc(post_ld[2], 16)
                sp.dma_start(Wks[:, :, :], Wk.rearrange(rows, p=P)).then_inc(post_ld[2], 16)
                sp.dma_start(oW[:, :, :], out_W.rearrange(rows, p=P)).then_inc(post_ld[2], 16)
                sp.dma_start(qvbias[:, 0:D], bq.partition_broadcast(P)).then_inc(post_ld[2], 16)
                sp.dma_start(qvbias[:, D:2 * D], bv.partition_broadcast(P)).then_inc(post_ld[2], 16)
                for h in range(2):
                    sp.wait_ge(resid_done, b * 24 + 16 + 4 * (h + 1))
                    sp.dma_start(out_v[b, :, h * 4:h * 4 + 4, :], xs[:, h * 4:h * 4 + 4, :]).then_inc(x_st, 16)
            sp.wait_ge(x_st, B * 32 + DMA_CREDIT)

        @block.gpsimd
        def _(pool):
            g_ = nc.gpsimd
            g_.memset(ident[:, :], 0.0).then_inc(mask_a, 1)
            g_.memset(blockdiag[:, :], 1.0).then_inc(mask_a, 1)
            g_.memset(ones[:, :], 1.0).then_inc(mask_a, 1)
            g_.memset(nhalf[:, :], -0.5).then_inc(mask_a, 1)
            pool.wait_ge(mask_a, 4)
            g_.affine_select(out=ident[:, :], in_=ident[:, :], compare_op=ALU.not_equal, fill=1.0, base=0,
                             pattern=[[-1, P]], channel_multiplier=1).then_inc(mask_b, 1)
            bd = blockdiag[:, :].rearrange("p (c l) -> p c l", l=DH1)
            g_.affine_select(out=bd, in_=bd, compare_op=ALU.is_ge, fill=0.0, base=0,
                             pattern=[[-DH1, P // DH1], [0, DH1]], channel_multiplier=1).then_inc(mask_b, 1)
            pool.wait_ge(mask_b, 2)
            g_.affine_select(out=bd, in_=bd, compare_op=ALU.is_ge, fill=0.0, base=DH1 - 1,
                             pattern=[[DH1, P // DH1], [0, DH1]], channel_multiplier=-1).then_inc(consts, 1)

            def layer_norm(b, k):
                for h in range(2):
                    n = b * 8 + k * 2 + h
                    hs = slice(h * 4, h * 4 + 4)
                    wait_alone(pool, mv_done, n + 1, tick)
                    g_.tensor_scalar(veps[:, hs], mv[:, hs, 1], EPS, 1.0, ALU.add, ALU.mult).then_inc(veps_done, 1)
                    pool.wait_ge(veps_done, n + 1)
                    g_.tensor_tensor(rstd[:, hs], veps[:, hs], nhalf[:, :], ALU.pow).then_inc(rstd_done, 1)

            def split_w(b, p):
                g = b * PAIRS + p
                pool.wait_ge(w_ld, 32 * (g + 1))
                wait_alone(pool, vT_done, 2 * g + 1, tick)
                g_.tensor_copy(wh[:, :, :, :], wraw[:, :, :, :]).then_inc(wh_done, 1)
                pool.wait_ge(wh_done, g + 1)
                g_.tensor_tensor(wl[:, :, :, :], wraw[:, :, :, :], wh[:, :, :, :].bitcast(F32),
                                 ALU.subtract).then_inc(w_done, 1)

            with pool.Fori(0, B) as b:
                layer_norm(b, 0)
                for h in range(2):
                    for k in range(KD):
                        i = h * 2 + k
                        wait_alone(pool, lnT_done, b * 16 + i + 1, tick)
                        g_.tensor_copy(xnh[:, k, h * CH:(h + 1) * CH],
                                       xT[:, k, h * CH:(h + 1) * CH]).then_inc(xnh_done, 1)
                split_w(b, 0)

                def pair(p, par):
                    last = isinstance(p, int) and p == PAIRS - 1
                    if not last:
                        split_w(b, p + 1)
                    g = b * PAIRS + p
                    for s in range(STEPS):
                        c, t = divmod(s, TT)
                        if t == 0:
                            pool.wait_ge(sum_full, g * 2 + c - 1 + SUM_CREDIT)
                            continue
                        n = (g * 2 + c) * (TT - 1) + t
                        pool.wait_ge(exp_done, g * STEPS + s + 1 + EXP_CREDIT)
                        if t > 1:
                            pool.wait_ge(presum_done, n - 1 + PRESUM_CREDIT)
                        other = pb[:, (s - 1) % 4, :, :] if t == 1 else acc[:, c, :, :]
                        g_.tensor_tensor(acc[:, c, :, :], other, pb[:, s % 4, :, :],
                                         ALU.add).then_inc(presum_done, 1)

                for_pairs(pool, pair)
                for k in range(1, 4):
                    layer_norm(b, k)

        @block.vector
        def _(dve):
            v = nc.vector
            for s, n in ((exp_done, EXP_CREDIT), (pv_done, PV_CREDIT), (st_full, ST_CREDIT),
                         (presum_done, PRESUM_CREDIT), (sum_full, SUM_CREDIT), (asm_ld, DMA_CREDIT),
                         (m_ld, DMA_CREDIT), (x_st, DMA_CREDIT), (ring_free[0], 1), (ring_free[1], 1),
                         (small_free, 1), (mT_full, 1), (o_free, 1), (norm_done, 1), (y_free, 2),
                         (w_done, 1), (vT_done, 1), (qv_done, 4), (ya_done, 2)):
                dve.sem_inc(s, n)

            dve.wait_ge(silu_done, 1)
            n = 0
            for b in range(B):
                for k in range(KD):
                    v.tensor_copy(scb[:, b, k, :], sc[:, b, k:k + 1].to_broadcast([P, P])).then_inc(scb_done, 1)
            dve.wait_ge(modps, 1)
            for b in range(B):
                v.tensor_tensor(mc[:, :, b], ps[:, 0, 0:32].rearrange("p (j b) -> p j b", b=B)[:, :, b],
                                cols[:, :], ALU.add).then_inc(mod_step, 1)
            dve.wait_ge(modps, 3)
            for b in range(B):
                v.tensor_tensor(gates[:, b, 0:2, :], ps[:, 1 + b, :].rearrange("p (g d) -> p g d", g=2),
                                gb[:, :, :], ALU.add).then_inc(mod_step, 1)
            dve.wait_ge(mod_step, 4)
            for b in range(B):
                v.tensor_scalar(affs[:, b, 0, 0, :], mc[:, 2:4, b], 1.0, None, ALU.add).then_inc(mod_done, 1)
                v.tensor_copy(affs[:, b, 1, 0, :], mc[:, 0:2, b]).then_inc(mod_done, 1)
                v.tensor_scalar(affs[:, b, 0, 1, :], mc[:, 8:10, b], 1.0, None, ALU.add).then_inc(mod_done, 1)
                v.tensor_copy(affs[:, b, 1, 1, :], mc[:, 6:8, b]).then_inc(mod_done, 1)
                v.tensor_copy(affs[:, b, 0, 2, :], lnp[:, 0, :]).then_inc(mod_done, 1)
                v.tensor_copy(affs[:, b, 1, 2, :], lnp[:, 1, :]).then_inc(mod_done, 1)
                v.tensor_scalar(mc[:, 12:14, b], mc[:, 12:14, b], 1.0, None, ALU.add).then_inc(mod_done, 1)
            dve.wait_ge(mod_done, 14)
            for b in range(B):
                v.tensor_tensor(affs[:, b, 0, 3, :], mc[:, 12:14, b], lnp[:, 2, :], ALU.mult).then_inc(mod_done, 1)
                v.tensor_tensor(affs[:, b, 1, 3, :], mc[:, 12:14, b], lnp[:, 3, :], ALU.mult).then_inc(mod_done, 1)
            dve.wait_ge(mod_done, 18)
            for b in range(B):
                v.tensor_tensor(affs[:, b, 1, 3, :], affs[:, b, 1, 3, :], mc[:, 14:16, b], ALU.add).then_inc(mod_done, 1)
            dve.wait_ge(mod_done, 20)

            def layer_norm(b, k, src, ready):
                for h in range(2):
                    n = b * 8 + k * 2 + h
                    ready(h)
                    for t in range(h * 4, h * 4 + 4):
                        i = v.bn_stats(stat[:, t, :], src[:, t, :])
                    i.then_inc(stat_done, 1)
                    wait_alone(dve, stat_done, n + 1, tick)
                    for t in range(h * 4, h * 4 + 4):
                        i = v.bn_aggr(mv[:, t, :], stat[:, t, :])
                    i.then_inc(mv_done, 1)
                for h in range(2):
                    n = b * 8 + k * 2 + h
                    dve.wait_ge(mv_done, n + 1)
                    dve.wait_ge(rstd_done, n + 1)
                    for t in range(h * 4, h * 4 + 4):
                        i = v.tensor_scalar(xh[:, t, :], src[:, t, :], mv[:, t, 0:1], rstd[:, t:t + 1],
                                            ALU.subtract, ALU.mult)
                    i.then_inc(xhat_done, 1)

            def residual(b, j0, gate):
                for t in range(TT):
                    j = b * 24 + j0 + t
                    dve.wait_ge(y_full, j + 1)
                    if j0 + t >= 2:
                        dve.wait_ge(resid_done, j - 1)
                    v.tensor_tensor(rtmp[:, t % 2, :], y_ps[t % 2], rowbias[:, gate, :], ALU.add).then_inc(y_free, 1)
                    dve.wait_ge(y_free, j + 1 + 2)
                    v.tensor_tensor(rtmp[:, t % 2, :], rtmp[:, t % 2, :], gates[:, bass.ds(b, 1), gate, :].rearrange("p o d -> p (o d)"),
                                    ALU.mult).then_inc(r_step, 1)
                    dve.wait_ge(r_step, j + 1)
                    v.tensor_tensor(xs[:, t, :], xs[:, t, :], rtmp[:, t % 2, :], ALU.add).then_inc(resid_done, 1)

            def normalise(b, p, c, used):
                g2 = (b * PAIRS + p) * 2 + c
                dve.wait_ge(sum_full, g2 + 1 + SUM_CREDIT)
                dve.wait_ge(norm_done, g2 + 1)
                v.reciprocal(rec[:, :], small_ps).then_inc(small_free, 1)
                dve.wait_ge(small_free, b * SMALL_B + used + 2)
                dve.wait_ge(o_free, g2 + 1 + 1)
                v.tensor_tensor(OT[:, bass.ds(p, 1), c * CH:(c + 1) * CH].rearrange("p o n -> p (o n)"), o_raw[:, :], rec[:, :],
                                ALU.mult).then_inc(norm_done, 1)

            def side(b, p, item, r):
                if item[0] == "proj":
                    k = item[1]
                    bank, before = r.take()
                    if k < 4:
                        dst, lead = (ql, qh) if k % 2 == 0 else (kl, kh)
                        cs = slice((k // 2) * CH, (k // 2 + 1) * CH)
                        dve.wait_ge(lead_done, (b * PAIRS + p) * 4 + k + 1)
                        v.tensor_tensor(dst[:, cs], ring[bank], lead[:, cs].bitcast(F32),
                                        ALU.subtract).then_inc(ring_free[bank], 1)
                        dve.wait_ge(ring_free[bank], before + 2)
                        dve.sem_inc(rest_done, 1)
                elif item[0] == "vt":
                    r.take()
                elif item[0] == "max":
                    taken = []
                    for kc in range(2):
                        bank, before = r.take()
                        taken.append((bank, before))
                        dve.wait_ge(ring_full[bank], before + 1)
                        v.tensor_reduce(mpart[:, item[2], kc:kc + 1], ring[bank], AX.X,
                                        ALU.max).then_inc(ring_free[bank], 1)
                    if item[2] == 7:
                        n = (b * PAIRS + p) * 2 + item[1]
                        for bank, before in taken:
                            dve.wait_ge(ring_free[bank], before + 2)
                        v.tensor_reduce(mx[:, :], mpart[:, :, :], AX.X, ALU.max).then_inc(mx_step, 1)
                        dve.wait_ge(mx_step, 3 * n + 1)
                        dve.wait_ge(mT_full, n + 1)
                        mx_v = mx[:, :].rearrange("p (h t) -> p t h", h=2)
                        v.tensor_copy(ml[:, :, :, 0], mx_v).then_inc(mx_step, 1)
                        dve.wait_ge(mx_step, 3 * n + 2)
                        v.tensor_tensor(ml[:, :, :, 1], mx_v, ml[:, :, :, 0].bitcast(F32),
                                        ALU.subtract).then_inc(mx_step, 1)

            with dve.Fori(0, B) as b:
                v.tensor_copy(aff[:, :, :, :], affs[:, bass.ds(b, 1), :, :, :].rearrange("p o a k j -> p (o a) k j")).then_inc(aff_done, 1)
                layer_norm(b, 0, xs, lambda h: dve.wait_ge(x_ld, b * 32 + 32))
                for h in range(2):
                    for k in range(KD):
                        dve.wait_ge(xnh_done, b * 4 + h * 2 + k + 1)
                        cs = slice(h * CH, (h + 1) * CH)
                        v.tensor_tensor(xnl[:, k, cs], xT[:, k, cs], xnh[:, k, cs].bitcast(F32),
                                        ALU.subtract).then_inc(xnl_done, 1)
                for i in range(2):
                    for h in range(2):
                        v.memset(km[i][h][DH:DH + 2, :].bitcast(F32), -1.0).then_inc(neg_done, 1)
                r = Ring(b * (RING_B // 2))
                for item in PROLOGUE:
                    side(b, 0, item, r)

                def pair(p, par):
                    r = Ring(b * (RING_B // 2) + RING_PRO // 2 + p * (RING_IT // 2))
                    for s in range(STEPS):
                        for of_next, *item in side_items(p, s):
                            if item[0] == "sum":
                                if item[1] == 1:
                                    normalise(b, p - 1, 1, p * 4)
                                else:
                                    normalise(b, p, 0, p * 4 + 2)
                            else:
                                side(b, p + 1 if of_next else p, item, r)

                for_pairs(dve, pair)
                normalise(b, PAIRS - 1, 1, SMALL_B - 1)

                residual(b, 0, 0)
                layer_norm(b, 1, xs, lambda h: dve.wait_ge(resid_done, b * 24 + 4 * h + 4))
                residual(b, 8, 1)
                layer_norm(b, 2, xs, lambda h: dve.wait_ge(resid_done, b * 24 + 8 + 4 * h + 4))
                for h in range(KD):
                    n = b * 6 + h * 3
                    dve.wait_ge(kt_full, b * 2 + h + 1)
                    v.tensor_reduce(kmx[:, h:h + 1], ps[:, 2 * h:2 * h + 2, :], AX.XY, ALU.max).then_inc(kb_step, 1)
                    dve.wait_ge(kb_step, n + 1)
                    v.tensor_tensor(ktmp[:, h:h + 1], kmx[:, h:h + 1], bkc[:, h:h + 1], ALU.add).then_inc(kb_step, 1)
                    dve.wait_ge(kb_step, n + 2)
                    v.tensor_tensor(knb[:, h:h + 1], bkc[:, h:h + 1], ktmp[:, h:h + 1], ALU.subtract).then_inc(kb_step, 1)
                for t in range(TT):
                    dve.wait_ge(qv_full, b * 8 + t + 1)
                    v.tensor_tensor(QV[:, t, :], ps[:, 4 + t % 4, :], qvbias[:, :], ALU.add).then_inc(qv_done, 1)
                for h in range(2):
                    ts = slice(h * 4, h * 4 + 4)
                    q = QV[:, ts, 0:D].rearrange("p t (h d) -> p t h d", d=DH1)
                    dve.wait_ge(qv_done, b * 8 + 4 * h + 4 + 4)
                    v.tensor_reduce(qmx[:, ts, :], q, AX.X, ALU.max).then_inc(q_step, 1)
                    dve.wait_ge(q_step, b * 6 + h + 1)
                    v.tensor_tensor(q, q, qmx[:, ts, :].unsqueeze(3).to_broadcast([P, 4, H1, DH1]),
                                    ALU.subtract).then_inc(qsub_done, 1)
                for h in range(2):
                    ts = slice(h * 4, h * 4 + 4)
                    q = QV[:, ts, 0:D].rearrange("p t (h d) -> p t h d", d=DH1)
                    dve.wait_ge(qexp_done, b * 2 + h + 1)
                    v.tensor_reduce(qsum[:, ts, :], q, AX.X, ALU.add).then_inc(q_step, 1)
                    dve.wait_ge(q_step, b * 6 + 2 + 2 * h + 1)
                    v.reciprocal(qrs[:, ts, :], qsum[:, ts, :]).then_inc(q_step, 1)
                    dve.wait_ge(q_step, b * 6 + 2 + 2 * h + 2)
                    v.tensor_tensor(q, q, qrs[:, ts, :].unsqueeze(3).to_broadcast([P, 4, H1, DH1]),
                                    ALU.mult).then_inc(q_done, 1)
                dve.wait_ge(ke_done, b * 2 + 2)
                v.reciprocal(krs, ksum).then_inc(krs_done, 1)
                dve.wait_ge(krs_done, b + 1)
                for h in range(KD):
                    dve.wait_ge(ctx_full, b * 2 + h + 1)
                    v.scalar_tensor_tensor(cm[:, h, :], ps[:, 6 + h, 0:P], krs[:, h:h + 1], blockdiag[:, :],
                                           ALU.mult, ALU.mult).then_inc(ctx_done, 1)
                layer_norm(b, 3, Y, lambda h: dve.wait_ge(ya_done, b * 8 + 4 * h + 4 + 2))
                residual(b, 16, 2)

        @block.scalar
        def _(act):
            a = nc.scalar
            act.wait_ge(const_ld, 16 * N_CONST_DMAS)
            a.activation(sc[:, :, :], cT[:, :, :], ACT.Silu).then_inc(silu_done, 1)

            def layer_norm(b, k, func):
                for h in range(2):
                    for j in range(KD):
                        n = b * 16 + k * 4 + h * 2 + j
                        act.wait_ge(lnT_full, n + 1)
                        a.activation(xT[:, j, h * CH:(h + 1) * CH], ps[:, 2 * h + j, :], func,
                                     bias=aff[:, 1, k, j:j + 1], scale=aff[:, 0, k, j:j + 1]).then_inc(lnT_done, 1)

            def side(b, p, par, item, r, used):
                g = b * PAIRS + p
                if item[0] == "proj":
                    k = item[1]
                    bank, before = r.take()
                    act.wait_ge(ring_full[bank], before + 1)
                    cs = slice((k // 2) * CH, (k // 2 + 1) * CH)
                    if k == 0:
                        act.wait_ge(asm_ld, g * 384 + DMA_CREDIT)
                    if k < 4:
                        lead = qh if k % 2 == 0 else kh
                        a.copy(lead[:, cs], ring[bank]).then_inc(lead_done, 1)
                    else:
                        c = k - 4
                        a.copy(vT[:, c * CH:(c + 1) * CH], ring[bank]).then_inc(vT_done, 1)
                        act.wait_ge(vT_done, 2 * g + c + 1 + 1)
                        act.sem_inc(ring_free[bank], 1)
                elif item[0] == "vt":
                    c = item[1]
                    bank, before = r.take()
                    act.wait_ge(ring_full[bank], before + 1)
                    if c == 0:
                        act.wait_ge(pv_done, g * STEPS + PV_CREDIT - STEPS)
                    a.copy(vn[par][:, c * 4:c * 4 + 4, :],
                           ring[bank].rearrange("p (t n) -> p t n", n=P)).then_inc(ring_free[bank], 1)
                elif item[0] == "max":
                    r.take()
                    r.take()
                elif item[0] == "m":
                    n = g * 2 + item[1]
                    act.wait_ge(mT_full, n + 1 + 1)
                    act.wait_ge(m_ld, 32 * n + DMA_CREDIT)
                    a.copy(mrow[:, :], small_ps[0:4, :]).then_inc(small_free, 1)

            def take_output(b, p, c):
                g = b * PAIRS + p
                act.wait_ge(pv_done, g * STEPS + (c + 1) * TT + PV_CREDIT)
                act.wait_ge(norm_done, g * 2 + c + 1)
                a.copy(o_raw[:, :], o_ps).then_inc(o_free, 1)

            with act.Fori(0, B) as b:
                act.wait_ge(aff_done, b + 1)
                layer_norm(b, 0, ACT.Identity)
                r = Ring(b * (RING_B // 2))
                for item in PROLOGUE:
                    side(b, 0, 0, item, r, 0)

                def pair(p, par):
                    r = Ring(b * (RING_B // 2) + RING_PRO // 2 + p * (RING_IT // 2))
                    g = b * PAIRS + p
                    for s in range(STEPS):
                        S = g * STEPS + s
                        act.wait_ge(st_full, S + 1 + ST_CREDIT)
                        act.wait_ge(pv_done, S - 3 + PV_CREDIT)
                        c, t = divmod(s, TT)
                        done = (g * 2 + c) * (TT - 1) + t - 4 if t > 4 else \
                            (g * 2 + c) * (TT - 1) + 1 if t == 4 else (g * 2 + c - 1) * (TT - 1) + t + 4
                        act.wait_ge(presum_done, done + PRESUM_CREDIT)
                        a.activation(pb[:, s % 4, :, :], st[s % 2], ACT.Exp, scale=DH ** -0.5).then_inc(exp_done, 1)
                        if s == TT:
                            take_output(b, p, 0)
                        for of_next, *item in side_items(p, s):
                            if item[0] != "sum":
                                side(b, p + 1 if of_next else p, 1 - par if of_next else par, item, r, 0)
                    take_output(b, p, 1)

                for_pairs(act, pair)

                layer_norm(b, 1, ACT.Identity)
                for c in range(NC):
                    for m in range(MB):
                        n = b * 16 + c * MB + m
                        act.wait_ge(h_full, n + 1)
                        a.activation(OT[:, m, c * CH:(c + 1) * CH], ps[:, m % 4, :], ACT.Gelu,
                                     bias=b1c[:, m:m + 1]).then_inc(gelu_done, 1)
                layer_norm(b, 2, ACT.Identity)
                for h in range(KD):
                    act.wait_ge(kb_step, b * 6 + h * 3 + 3)
                    a.activation(KE[:, h, :], ps[:, 2 * h:2 * h + 2, :].rearrange("p c n -> p (c n)"), ACT.Exp,
                                 bias=knb[:, h:h + 1], accum_out=ksum[:, h:h + 1]).then_inc(ke_done, 1)
                for h in range(2):
                    act.wait_ge(qsub_done, b * 2 + h + 1)
                    a.activation(QV[:, h * 4:h * 4 + 4, 0:D], QV[:, h * 4:h * 4 + 4, 0:D], ACT.Exp).then_inc(qexp_done, 1)
                for h in range(KD):
                    for c in range(2):
                        act.wait_ge(kn_full, b * 4 + h * 2 + c + 1)
                        a.copy(KN[:, c * 4:c * 4 + 4, h * P:(h + 1) * P],
                               ps[:, 2 * h + c, :].rearrange("p (t n) -> p t n", n=P)).then_inc(kn_done, 1)
                for h in range(KD):
                    for c in range(2):
                        act.wait_ge(qt_full, b * 4 + h * 2 + c + 1)
                        a.copy(QT[:, h, c * CH:(c + 1) * CH], ps[:, 2 * h + c, :]).then_inc(qt_done, 1)
                for t in range(TT):
                    act.wait_ge(ya_full, b * 8 + t + 1)
                    a.copy(Y[:, t, :], y_ps[t % 2]).then_inc(ya_done, 1)
                layer_norm(b, 3, ACT.Silu)

        @block.tensor
        def _(pe):
            mm = nc.tensor.matmul

            pe.wait_ge(const_ld, 16 * N_CONST_DMAS)
            pe.wait_ge(silu_done, 1)
            for j in range(16):
                w = Wm if j < 12 else We
                col = (j if j < 12 else j - 12) * P
                for k in range(KD):
                    i = mm(ps[:, 0, 2 * j:2 * j + 2], w[:, k, col:col + P], sc[:, :, k], start=(k == 0), stop=(k == KD - 1))
            i.then_inc(modps, 1)
            pe.wait_ge(scb_done, 4)
            for b in range(B):
                for n, first in ((0, 2 * D), (1, 5 * D)):
                    for k in range(KD):
                        i = mm(ps[:, 1 + b, n * D:(n + 1) * D], scb[:, b, k, :], Wm[:, k, first:first + D],
                               start=(k == 0), stop=(k == KD - 1))
                i.then_inc(modps, 1)
            pe.wait_ge(consts, 1)
            pe.wait_ge(wo_ld, 16)

            def layer_norm(b, k):
                for h in range(2):
                    pe.wait_ge(xhat_done, b * 8 + k * 2 + h + 1)
                    for j in range(KD):
                        for t in range(4):
                            i = nc.tensor.transpose(ps[:, 2 * h + j, t * P:(t + 1) * P],
                                                    xh[:, h * 4 + t, j * P:(j + 1) * P], ident[:, :])
                        i.then_inc(lnT_full, 1)

            def side(b, p, par, item, r):
                g = b * PAIRS + p
                if item[0] == "proj":
                    k = item[1]
                    s = k % 2 if k < 4 else 2
                    c = k // 2 if k < 4 else k - 4
                    if k == 0:
                        pe.wait_ge(w_done, g + 1 + 1)
                    bank, before = r.take()
                    pe.wait_ge(ring_free[bank], before + 1)
                    cs = slice(c * CH, (c + 1) * CH)
                    n = 0
                    for kin in range(KD):
                        for w, xx in ((wh, xnh), (wh, xnl), (wl, xnh)):
                            i = mm(ring[bank], w[:, kin, s, :], xx[:, kin, cs], start=(n == 0), stop=(n == 5))
                            n += 1
                    i.then_inc(ring_full[bank], 1)
                elif item[0] == "vt":
                    c = item[1]
                    bank, before = r.take()
                    pe.wait_ge(ring_free[bank], before + 1)
                    pe.wait_ge(vT_done, 2 * g + c + 1 + 1)
                    for t in range(4):
                        n = c * 4 + t
                        i = nc.tensor.transpose(ring[bank][:, t * P:(t + 1) * P], vT[:, n * P:(n + 1) * P], ident[:, :])
                    i.then_inc(ring_full[bank], 1)
                elif item[0] == "max":
                    c, u = item[1], item[2]
                    h, t = divmod(u, TPC)
                    qs = slice(c * CH + t * P, c * CH + (t + 1) * P)
                    if c == 0 and u == 0:
                        pe.wait_ge(asm_ld, (g + 1) * 384 + DMA_CREDIT)
                    for kc in range(2):
                        bank, before = r.take()
                        ks = slice(kc * CH, (kc + 1) * CH)
                        pe.wait_ge(ring_free[bank], before + 1)
                        mm(ring[bank], qq[par][h][:, qs], kk[par][h][:, ks], start=True, stop=False)
                        mm(ring[bank], qm[par][h][0:DH, qs], km[par][h][0:DH, ks], start=False,
                           stop=True).then_inc(ring_full[bank], 1)
                elif item[0] == "m":
                    n = g * 2 + item[1]
                    pe.wait_ge(mx_step, 3 * (n + 1))
                    for t in range(TPC):
                        i = nc.tensor.transpose(small_ps[0:4, t * P:(t + 1) * P],
                                                ml[:, t, :, :].bitcast(F32).rearrange("p h a -> p (h a)"), ident[:, :])
                    i.then_inc(mT_full, 1)

            def row_sums(b, p, c, used):
                g2 = (b * PAIRS + p) * 2 + c
                pe.wait_ge(presum_done, (g2 + 1) * (TT - 1) + PRESUM_CREDIT)
                pe.wait_ge(small_free, b * SMALL_B + used + 1)
                for h in range(2):
                    i = mm(small_ps[h * DH:(h + 1) * DH, :], ones[:, :], acc[:, c, h, :], start=True, stop=True)
                i.then_inc(sum_full, 1)

            def pv(b, p, par, s):
                S = (b * PAIRS + p) * STEPS + s
                c, t = divmod(s, TT)
                pe.wait_ge(exp_done, S + 1 + EXP_CREDIT)
                if t == 0:
                    pe.wait_ge(o_free, (b * PAIRS + p) * 2 + c + 1)
                for h in range(2):
                    hs = slice(h * DH, (h + 1) * DH)
                    i = mm(o_ps[hs, :], vn[par][:, t, hs], pb[:, s % 4, h, :], start=(t == 0), stop=(t == TT - 1))
                i.then_inc(pv_done, 1)

            def products(b, j0, lhs, rhs, n):
                for t in range(TT):
                    j = b * 24 + j0 + t
                    pe.wait_ge(y_free, j + 1)
                    for k in range(n):
                        i = mm(y_ps[t % 2], lhs[:, k, t * P:(t + 1) * P], rhs[:, k, :], start=(k == 0), stop=(k == n - 1))
                    i.then_inc(y_full, 1)

            with pe.Fori(0, B) as b:
                layer_norm(b, 0)
                pe.wait_ge(xnl_done, b * 4 + 4)
                pe.wait_ge(neg_done, b * 4 + 4)
                r = Ring(b * (RING_B // 2))
                for item in PROLOGUE:
                    if item[0] == "m":
                        pe.wait_ge(small_free, b * SMALL_B + 1)
                    side(b, 0, 0, item, r)

                def pair(p, par):
                    g = b * PAIRS + p
                    r = Ring(b * (RING_B // 2) + RING_PRO // 2 + p * (RING_IT // 2))
                    for s in range(STEPS):
                        c, t = divmod(s, TT)
                        S = g * STEPS + s
                        if t == 0:
                            pe.wait_ge(m_ld, (g * 2 + c + 1) * 32 + DMA_CREDIT)
                        pe.wait_ge(exp_done, S - 1 + EXP_CREDIT)
                        ks, qs = slice(t * P, (t + 1) * P), slice(c * CH, (c + 1) * CH)
                        for h in range(2):
                            mm(st[s % 2][:, h, :], kk[par][h][:, ks], qq[par][h][:, qs], start=True, stop=False)
                            i = mm(st[s % 2][:, h, :], km[par][h][0:DH + 2, ks], qm[par][h][0:DH + 2, qs],
                                   start=False, stop=True)
                        i.then_inc(st_full, 1)
                        if s > 0:
                            pv(b, p, par, s - 1)
                        for of_next, *item in side_items(p, s):
                            if item == ["sum", 1]:
                                row_sums(b, p - 1, 1, p * 4)
                            elif item == ["sum", 0]:
                                row_sums(b, p, 0, p * 4 + 2)
                            else:
                                if item[0] == "m":
                                    pe.wait_ge(small_free, b * SMALL_B + p * 4 + (1 if item[1] else 3) + 1)
                                side(b, p + 1 if of_next else p, 1 - par if of_next else par, item, r)
                    pv(b, p, par, STEPS - 1)

                for_pairs(pe, pair)
                row_sums(b, PAIRS - 1, 1, SMALL_B - 1)

                pe.wait_ge(norm_done, (b + 1) * PAIRS * 2 + 1)
                products(b, 0, OT, Wo, PAIRS)
                layer_norm(b, 1)
                pe.wait_ge(lnT_done, b * 16 + 8)
                pe.wait_ge(post_ld[0], 16 * (b + 1))
                for c in range(NC):
                    for m in range(MB):
                        n = c * MB + m
                        if n >= 4:
                            pe.wait_ge(gelu_done, b * 16 + n - 3)
                        for k in range(KD):
                            i = mm(ps[:, m % 4, :], W1s[:, k, m * P:(m + 1) * P], xT[:, k, c * CH:(c + 1) * CH],
                                   start=(k == 0), stop=(k == KD - 1))
                        i.then_inc(h_full, 1)
                pe.wait_ge(gelu_done, b * 16 + 16)
                pe.wait_ge(post_ld[1], 16 * (b + 1))
                products(b, 8, OT, W2s, MB)
                layer_norm(b, 2)
                pe.wait_ge(lnT_done, b * 16 + 12)
                pe.wait_ge(post_ld[2], 96 * (b + 1))
                for h in range(KD):
                    for c in range(NC):
                        for k in range(KD):
                            i = mm(ps[:, 2 * h + c, :], Wks[:, k, h * P:(h + 1) * P], xT[:, k, c * CH:(c + 1) * CH],
                                   start=(k == 0), stop=(k == KD - 1))
                    i.then_inc(kt_full, 1)
                for t in range(TT):
                    pe.wait_ge(qv_done, b * 8 + t + 1)
                    for k in range(KD):
                        i = mm(ps[:, 4 + t % 4, :], xT[:, k, t * P:(t + 1) * P], Wqv[:, k, :],
                               start=(k == 0), stop=(k == KD - 1))
                    i.then_inc(qv_full, 1)
                for h in range(KD):
                    pe.wait_ge(ke_done, b * 2 + h + 1)
                    for c in range(2):
                        for t in range(4):
                            n = c * 4 + t
                            i = nc.tensor.transpose(ps[:, 2 * h + c, t * P:(t + 1) * P], KE[:, h, n * P:(n + 1) * P], ident[:, :])
                        i.then_inc(kn_full, 1)
                pe.wait_ge(kn_done, b * 4 + 4)
                pe.wait_ge(qv_done, b * 8 + 8 + 4)
                for h in range(KD):
                    for t in range(TT):
                        i = mm(ps[:, 6 + h, 0:P], KN[:, t, h * P:(h + 1) * P], QV[:, t, D + h * P:D + (h + 1) * P],
                               start=(t == 0), stop=(t == TT - 1))
                    i.then_inc(ctx_full, 1)
                pe.wait_ge(q_done, b * 2 + 2)
                for h in range(KD):
                    for c in range(2):
                        for t in range(4):
                            n = c * 4 + t
                            i = nc.tensor.transpose(ps[:, 2 * h + c, t * P:(t + 1) * P], QV[:, n, h * P:(h + 1) * P], ident[:, :])
                        i.then_inc(qt_full, 1)
                pe.wait_ge(qt_done, b * 4 + 4)
                pe.wait_ge(ctx_done, b * 2 + 2)
                for t in range(TT):
                    pe.wait_ge(ya_done, b * 8 + t + 1)
                    for h in range(KD):
                        i = mm(y_ps[t % 2][:, h * P:(h + 1) * P], QT[:, h, t * P:(t + 1) * P], cm[:, h, :], start=True, stop=True)
                    i.then_inc(ya_full, 1)
                layer_norm(b, 3)
                pe.wait_ge(lnT_done, b * 16 + 16)
                products(b, 16, xT, oW, KD)


N_CONST_DMAS = 18

_INS = ['x', 'cond_1024', 'L0_cond_W_mod', 'L0_cond_b_mod', 'L0_cond_W_qkv', 'L0_cond_W_out', 'L0_cond_b_out',
        'L0_cond_W1', 'L0_cond_b1', 'L0_cond_W2', 'L0_cond_b2', 'L1_cond_norm_g', 'L1_cond_norm_b', 'L1_cond_Wq',
        'L1_cond_bq', 'L1_cond_Wk', 'L1_cond_bk', 'L1_cond_Wv', 'L1_cond_bv', 'L1_cond_emb_W', 'L1_cond_emb_b',
        'L1_cond_sn_g', 'L1_cond_sn_b', 'L1_cond_out_W', 'L1_cond_out_b']
_OUTS = [((2, 1024, 256), 'float32')]


def kernel(**inputs):
    import numpy as _np
    import concourse.bacc as _bacc
    from concourse import mybir as _mybir
    from concourse.bass_utils import run_bass_kernel_spmd as _run

    nc = _bacc.Bacc("TRN2", target_bir_lowering=False, num_devices=1)
    arrays, args = {}, []
    for name in _INS:
        a = _np.ascontiguousarray(inputs[name])
        arrays[f"in_{name}_dram"] = a
        args.append(nc.dram_tensor(f"in_{name}_dram", a.shape, _mybir.dt.from_np(a.dtype), kind="ExternalInput").ap())
    for i, (shape, dtype) in enumerate(_OUTS):
        dt = _mybir.dt.from_np(_np.dtype(dtype))
        args.append(nc.dram_tensor(f"out_{i}_dram", shape, dt, kind="ExternalOutput").ap())
    dit_kernel(nc, *args)
    r = _run(nc, [arrays], core_ids=[0])
    got = tuple(r.results[0][f"out_{i}_dram"] for i in range(len(_OUTS)))
    return got[0]
```

```python
from contextlib import ExitStack

import concourse.bass as bass
from concourse import mybir

F32 = mybir.dt.float32
F32R = mybir.dt.float32r
ACT = mybir.ActivationFunctionType
ALU = mybir.AluOpType
AX = mybir.AxisListType

P = 128
B, T, D = 2, 1024, 256
KD = D // P
TT = T // P
CH = 512
NC = T // CH
TPC = CH // P
HEADS, DH = 16, 64
PAIRS = HEADS // 2
MLP = 1024
MB = MLP // P
H1, DH1 = 16, 16
EPS = 1e-5
STEPS = NC * TT

ST_CREDIT = STEPS + 1
EXP_CREDIT = 2
PV_CREDIT = STEPS + 4
PRESUM_CREDIT = TT - 1
SUM_CREDIT = 2
DMA_CREDIT = 16

RING_PRO = 6 + 2 + 16
RING_IT = 16 + RING_PRO
RING_B = RING_PRO + (PAIRS - 1) * RING_IT + 16
SMALL_B = 4 * PAIRS

SIDE = {
    0: [("max", 1, 0), ("max", 1, 1)],
    1: [("max", 1, 2), ("max", 1, 3)],
    2: [("max", 1, 4), ("proj", 0)],
    3: [("max", 1, 5), ("proj", 1)],
    4: [("max", 1, 6), ("proj", 2)],
    5: [("max", 1, 7), ("proj", 3)],
    6: [("proj", 4), ("m", 1)],
    7: [("sum", 1), ("proj", 5)],
    8: [("max", 0, 0)],
    9: [("max", 0, 1), ("sum", 0)],
    10: [("vt", 0), ("max", 0, 2)],
    11: [("max", 0, 3), ("max", 0, 4)],
    12: [("max", 0, 5), ("max", 0, 6)],
    13: [("max", 0, 7)],
    14: [("vt", 1), ("m", 0)],
    15: [],
}
PROLOGUE = [("proj", k) for k in (0, 1, 4, 2, 3, 5)] + [("vt", 0), ("vt", 1)] \
    + [("max", 0, u) for u in range(8)] + [("m", 0)]


def small_use(p, item):
    if item == ("m", 1) and isinstance(p, int) and p == 0:
        return 1
    return p * 4 + {("m", 1): 0, ("sum", 1): 1, ("sum", 0): 2, ("m", 0): 3}[item]


def side_items(p, s):
    out = []
    for item in SIDE[s]:
        of_next = item[0] in ("proj", "vt") or item[0] in ("max", "m") and item[1] == 0
        if of_next and isinstance(p, int) and p == PAIRS - 1:
            continue
        if item == ("sum", 1) and isinstance(p, int) and p == 0:
            continue
        out.append((of_next,) + item)
    return out


def wait_alone(eng, sem, value, tick):
    eng.wait_ge(sem, value)
    eng.sem_inc(tick, 1)


class Ring:

    def __init__(self, base):
        self.base, self.k = base, 0

    def take(self):
        bank, before = self.k % 2, self.base + self.k // 2
        self.k += 1
        return bank, before


def for_pairs(eng, emit):
    emit(0, 0)
    with eng.Fori(0, (PAIRS - 2) // 2) as two:
        emit(two * 2 + 1, 1)
        emit(two * 2 + 2, 0)
    emit(PAIRS - 1, 1)


def dit_kernel(nc, x, cond, W_mod, b_mod, W_qkv, W_out, b_out, W1, b1, W2, b2,
               norm_g, norm_b, Wq, bq, Wk, bk, Wv, bv, emb_W, emb_b, sn_g, sn_b, out_W, out_b, out):
    with ExitStack() as ctx:
        place = [(nc.sbuf_base + 31) // 32 * 32]

        def at(name, shape, dt, offset):
            return nc.alloc_sbuf_tensor_at(name, shape, dt, offset=offset)

        def sb(name, shape, dt=F32):
            n = 4
            for s in shape[1:]:
                n *= s
            t = at(name, shape, dt, place[0])
            place[0] += (n + 31) // 32 * 32
            return t

        def sem(name):
            return ctx.enter_context(nc.semaphore(name))

        ident = sb("ident", [P, P])
        ones = sb("ones", [P, DH])
        blockdiag = sb("blockdiag", [P, P])
        gates = sb("gates", [P, B, 3, D])
        rowbias = sb("rowbias", [P, 3, D])
        affs = sb("affs", [P, B, 2, 4, KD])
        aff = sb("aff", [P, 2, 4, KD])
        b1c = sb("b1c", [P, MB])
        bkc = sb("bkc", [P, KD])
        nhalf = sb("nhalf", [P, TPC])
        small = sb("small", [P, 64])
        ktmp, knb, ksum, krs = small[:, 0:2], small[:, 2:4], small[:, 4:6], small[:, 6:8]
        kmx = small[:, 8:10]
        stat = sb("stat", [P, TT, 6])
        mv = sb("mv", [P, TT, 2])
        veps = sb("veps", [P, TT])
        rstd = sb("rstd", [P, TT])
        xs = sb("xs", [P, TT, D])
        xnh = sb("xnh", [P, KD, T], F32R)
        xnl = sb("xnl", [P, KD, T], F32R)
        OT = sb("OT", [P, PAIRS, T])
        Wo = sb("Wo", [P, PAIRS, D])
        wraw = sb("wraw", [P, KD, 3, P])
        wh = sb("wh", [P, KD, 3, P], F32R)
        wl = sb("wl", [P, KD, 3, P], F32R)
        vn = [sb(f"vn{i}", [P, TT, P]) for i in range(2)]
        vT0 = place[0]
        vT = sb("vT", [P, T])
        cm = at("cm", [P, KD, P], F32, vT0)
        qmx = at("qmx", [P, TT, H1], F32, vT0 + 1024)
        qsum = at("qsum", [P, TT, H1], F32, vT0 + 1536)
        qrs = at("qrs", [P, TT, H1], F32, vT0 + 2048)
        acc = sb("acc", [P, NC, 2, CH])
        rtmp = at("rtmp", [P, 2, D], F32, place[0])
        o_raw = sb("o_raw", [P, CH])
        rec = sb("rec", [P, CH])
        mpart = sb("mpart", [P, 8, 2])
        mx = sb("mx", [P, 8])
        ml = sb("ml", [P, TPC, 2, 2], F32R)
        mrow = sb("mrow", [4, CH], F32R)
        pb0 = place[0]
        pb = sb("pb", [P, 4, 2, CH])
        xh = at("xh", [P, TT, D], F32, pb0)
        xT = at("xT", [P, KD, T], F32, pb0 + 8192)
        sg0 = place[0]
        qh = sb("qh", [P, T], F32R)
        ql = sb("ql", [P, T], F32R)
        kh = sb("kh", [P, T], F32R)
        kl = sb("kl", [P, T], F32R)
        Wqv = at("Wqv", [P, KD, 2 * D], F32, sg0)
        Wks = at("Wks", [P, KD, D], F32, sg0 + 4096)
        oW = at("oW", [P, KD, D], F32, sg0 + 6144)
        qvbias = at("qvbias", [P, 2 * D], F32, sg0 + 8192)
        k0 = place[0]
        qq = [[sb(f"qq{i}{h}", [P, T], F32R) for h in range(2)] for i in range(2)]
        kk = [[sb(f"kk{i}{h}", [P, T], F32R) for h in range(2)] for i in range(2)]
        qm = [[sb(f"qm{i}{h}", [P, T], F32R) for h in range(2)] for i in range(2)]
        km = [[sb(f"km{i}{h}", [P, T], F32R) for h in range(2)] for i in range(2)]
        assert place[0] <= nc.sbuf_usable_end, place[0]
        W1s = at("W1s", [P, KD, MLP], F32, k0)
        W2s = at("W2s", [P, MB, D], F32, k0 + 8192)
        KE = at("KE", [P, KD, T], F32, k0 + 16384)
        KN = at("KN", [P, TT, D], F32, k0 + 24576)
        QV = at("QV", [P, TT, 2 * D], F32, k0 + 32768)
        QT = at("QT", [P, KD, T], F32, k0 + 49152)
        Y = at("Y", [P, TT, D], F32, k0 + 57344)
        Wm = at("Wm", [P, KD, 6 * D], F32, k0)
        We = at("We", [P, KD, 2 * D], F32, k0 + 12288)
        cT = at("cT", [P, B, KD], F32, k0 + 16384)
        sc = at("sc", [P, B, KD], F32, k0 + 16384 + 32)
        cols = at("cols", [P, 16], F32, k0 + 16384 + 64)
        mc = at("mc", [P, 16, B], F32, k0 + 16384 + 128)
        lnp = at("lnp", [P, 4, KD], F32, k0 + 16384 + 256)
        gb = at("gb", [P, 2, D], F32, k0 + 16384 + 512)
        scb = at("scb", [P, B, KD, P], F32, k0 + 16384 + 4096)

        ps = ctx.enter_context(nc.psum_tensor("ps", [P, 8, 512], F32))
        st = [ps[:, 0:2, :], ps[:, 2:4, :]]
        o_ps = ps[:, 4, :]
        small_ps = ps[:, 5, :]
        ring = [ps[:, 6, :], ps[:, 7, :]]
        y_ps = [ps[:, 4 + n, 0:D] for n in range(4)]

        const_ld = sem("const_ld")
        tick = sem("tick")
        wo_ld = sem("wo_ld")
        mask_a, mask_b, consts = sem("mask_a"), sem("mask_b"), sem("consts")
        silu_done, scb_done, modps, mod_done, mod_step = (sem("silu_done"), sem("scb_done"), sem("modps"), sem("mod_done"), sem("mod_step"))
        aff_done = sem("aff_done")
        x_ld, x_st = sem("x_ld"), sem("x_st")
        stat_done, mv_done, veps_done, rstd_done, xhat_done = (
            sem("stat_done"), sem("mv_done"), sem("veps_done"), sem("rstd_done"), sem("xhat_done"))
        lnT_full, lnT_done, xnh_done, xnl_done = sem("lnT_full"), sem("lnT_done"), sem("xnh_done"), sem("xnl_done")
        w_ld, wh_done, w_done, neg_done = sem("w_ld"), sem("wh_done"), sem("w_done"), sem("neg_done")
        ring_full = [sem("ring_full0"), sem("ring_full1")]
        ring_free = [sem("ring_free0"), sem("ring_free1")]
        small_free, mT_full, sum_full = sem("small_free"), sem("mT_full"), sem("sum_full")
        lead_done, rest_done, vT_done, asm_ld = sem("lead_done"), sem("rest_done"), sem("vT_done"), sem("asm_ld")
        mx_step, m_ld = sem("mx_step"), sem("m_ld")
        st_full, exp_done, pv_done, presum_done = sem("st_full"), sem("exp_done"), sem("pv_done"), sem("presum_done")
        o_free, norm_done = sem("o_free"), sem("norm_done")
        y_full, y_free, r_step, resid_done = sem("y_full"), sem("y_free"), sem("r_step"), sem("resid_done")
        post_ld = [sem("w1_ld"), sem("w2_ld"), sem("l1_ld")]
        h_full, gelu_done = sem("h_full"), sem("gelu_done")
        kt_full, kb_step, ke_done, krs_done, kn_full, kn_done = (
            sem("kt_full"), sem("kb_step"), sem("ke_done"), sem("krs_done"), sem("kn_full"), sem("kn_done"))
        qv_full, qv_done, qsub_done, qexp_done, q_step, q_done = (
            sem("qv_full"), sem("qv_done"), sem("qsub_done"), sem("qexp_done"), sem("q_step"), sem("q_done"))
        qt_full, qt_done, ctx_full, ctx_done, ya_full, ya_done = (
            sem("qt_full"), sem("qt_done"), sem("ctx_full"), sem("ctx_done"), sem("ya_full"), sem("ya_done"))

        x_v = x.rearrange("b (t p) d -> b p t d", p=P)
        out_v = out.rearrange("b (t p) d -> b p t d", p=P)
        rows = "(k p) n -> p k n"
        wqkv_v = W_qkv.rearrange("(k p) (s n) -> k p s n", p=P, s=3)

        block = ctx.enter_context(nc.Block())

        @block.sync
        def _(sp):
            N_CONST = [0]

            def const(dst, src):
                sp.dma_start(dst, src).then_inc(const_ld, 16)
                N_CONST[0] += 1

            with nc.allow_non_contiguous_dma(reason="small vectors into columns"):
                const(cT[:, :, :], cond.rearrange("b (k p) -> p b k", p=P))
                const(cols[:, 0:12], b_mod.rearrange("(j p) -> p j", p=P))
                const(cols[:, 12:16], emb_b.rearrange("(j p) -> p j", p=P))
                for n, v in enumerate((norm_g, norm_b, sn_g, sn_b)):
                    const(lnp[:, n, :], v.rearrange("(j p) -> p j", p=P))
                const(b1c[:, :], b1.rearrange("(j p) -> p j", p=P))
                const(bkc[:, :], bk.rearrange("(j p) -> p j", p=P))
                const(Wm[:, :, :], W_mod.rearrange(rows, p=P))
                const(We[:, :, :], emb_W.rearrange(rows, p=P))
                const(gb[:, 0, :], b_mod[2 * D:3 * D].partition_broadcast(P))
                const(gb[:, 1, :], b_mod[5 * D:6 * D].partition_broadcast(P))
                for b in range(B):
                    const(gates[:, b, 2, :], cond[b, :].partition_broadcast(P))
                for n, v in enumerate((b_out, b2, out_b)):
                    const(rowbias[:, n, :], v.partition_broadcast(P))
            assert N_CONST[0] == N_CONST_DMAS
            sp.dma_start(Wo[:, :, :], W_out.rearrange(rows, p=P)).then_inc(wo_ld, 16)

            def load_w(b, p):
                g = b * PAIRS + p
                sp.wait_ge(w_done, g + 1)
                for k in range(KD):
                    sp.dma_start(wraw[:, k, :, :], wqkv_v[k, :, :, bass.ds(p * P, P)]).then_inc(w_ld, 16)

            def assemble(b, p, par, k):
                g = b * PAIRS + p
                cs = slice((k // 2) * CH, (k // 2 + 1) * CH)
                if k == 0:
                    sp.wait_ge(st_full, g * STEPS + ST_CREDIT - STEPS)
                sp.wait_ge(rest_done, g * 4 + k + 1)
                for h in range(2):
                    s = slice(h * DH, (h + 1) * DH)
                    if k % 2 == 0:
                        moves = [(qq[par][h][0:DH, cs], qh[s, cs]), (qm[par][h][0:DH, cs], qh[s, cs]),
                                 (qq[par][h][DH:P, cs], ql[s, cs])]
                    else:
                        moves = [(kk[par][h][0:DH, cs], kh[s, cs]), (kk[par][h][DH:P, cs], kh[s, cs]),
                                 (km[par][h][0:DH, cs], kl[s, cs])]
                    for dst, src in moves:
                        sp.dma_start(dst.bitcast(F32), src.bitcast(F32)).then_inc(asm_ld, 16)

            def max_rows(b, p, par, c, used):
                sp.wait_ge(small_free, b * SMALL_B + used + 2)
                for h in range(2):
                    sp.dma_start(qm[par][h][DH:DH + 2, c * CH:(c + 1) * CH].bitcast(F32),
                                 mrow[2 * h:2 * h + 2, :].bitcast(F32)).then_inc(m_ld, 16)

            with sp.Fori(0, B) as b:
                load_w(b, 0)
                for h in range(2):
                    sp.wait_ge(x_st, b * 32 + DMA_CREDIT)
                    sp.dma_start(xs[:, h * 4:h * 4 + 4, :], x_v[b, :, h * 4:h * 4 + 4, :]).then_inc(x_ld, 16)
                for k in range(4):
                    assemble(b, 0, 0, k)
                max_rows(b, 0, 0, 0, 0)

                def pair(p, par):
                    last = isinstance(p, int) and p == PAIRS - 1
                    if not last:
                        load_w(b, p + 1)
                        assemble(b, p + 1, 1 - par, 0)
                        assemble(b, p + 1, 1 - par, 1)
                        assemble(b, p + 1, 1 - par, 2)
                        assemble(b, p + 1, 1 - par, 3)
                    max_rows(b, p, par, 1, small_use(p, ("m", 1)))
                    if not last:
                        max_rows(b, p + 1, 1 - par, 0, p * 4 + 3)

                for_pairs(sp, pair)
                sp.wait_ge(st_full, (b + 1) * PAIRS * STEPS + ST_CREDIT)
                sp.dma_start(W1s[:, :, :], W1.rearrange(rows, p=P)).then_inc(post_ld[0], 16)
                sp.dma_start(W2s[:, :, :], W2.rearrange(rows, p=P)).then_inc(post_ld[1], 16)
                sp.dma_start(Wqv[:, :, 0:D], Wq.rearrange(rows, p=P)).then_inc(post_ld[2], 16)
                sp.dma_start(Wqv[:, :, D:2 * D], Wv.rearrange(rows, p=P)).then_inc(post_ld[2], 16)
                sp.dma_start(Wks[:, :, :], Wk.rearrange(rows, p=P)).then_inc(post_ld[2], 16)
                sp.dma_start(oW[:, :, :], out_W.rearrange(rows, p=P)).then_inc(post_ld[2], 16)
                sp.dma_start(qvbias[:, 0:D], bq.partition_broadcast(P)).then_inc(post_ld[2], 16)
                sp.dma_start(qvbias[:, D:2 * D], bv.partition_broadcast(P)).then_inc(post_ld[2], 16)
                for h in range(2):
                    sp.wait_ge(resid_done, b * 24 + 16 + 4 * (h + 1))
                    sp.dma_start(out_v[b, :, h * 4:h * 4 + 4, :], xs[:, h * 4:h * 4 + 4, :]).then_inc(x_st, 16)
            sp.wait_ge(x_st, B * 32 + DMA_CREDIT)

        @block.gpsimd
        def _(pool):
            g_ = nc.gpsimd
            g_.memset(ident[:, :], 0.0).then_inc(mask_a, 1)
            g_.memset(blockdiag[:, :], 1.0).then_inc(mask_a, 1)
            g_.memset(ones[:, :], 1.0).then_inc(mask_a, 1)
            g_.memset(nhalf[:, :], -0.5).then_inc(mask_a, 1)
            pool.wait_ge(mask_a, 4)
            g_.affine_select(out=ident[:, :], in_=ident[:, :], compare_op=ALU.not_equal, fill=1.0, base=0,
                             pattern=[[-1, P]], channel_multiplier=1).then_inc(mask_b, 1)
            bd = blockdiag[:, :].rearrange("p (c l) -> p c l", l=DH1)
            g_.affine_select(out=bd, in_=bd, compare_op=ALU.is_ge, fill=0.0, base=0,
                             pattern=[[-DH1, P // DH1], [0, DH1]], channel_multiplier=1).then_inc(mask_b, 1)
            pool.wait_ge(mask_b, 2)
            g_.affine_select(out=bd, in_=bd, compare_op=ALU.is_ge, fill=0.0, base=DH1 - 1,
                             pattern=[[DH1, P // DH1], [0, DH1]], channel_multiplier=-1).then_inc(consts, 1)

            def layer_norm(b, k):
                for h in range(2):
                    n = b * 8 + k * 2 + h
                    hs = slice(h * 4, h * 4 + 4)
                    wait_alone(pool, mv_done, n + 1, tick)
                    g_.tensor_scalar(veps[:, hs], mv[:, hs, 1], EPS, 1.0, ALU.add, ALU.mult).then_inc(veps_done, 1)
                    pool.wait_ge(veps_done, n + 1)
                    g_.tensor_tensor(rstd[:, hs], veps[:, hs], nhalf[:, :], ALU.pow).then_inc(rstd_done, 1)

            def split_w(b, p):
                g = b * PAIRS + p
                pool.wait_ge(w_ld, 32 * (g + 1))
                wait_alone(pool, vT_done, 2 * g + 1, tick)
                g_.tensor_copy(wh[:, :, :, :], wraw[:, :, :, :]).then_inc(wh_done, 1)
                pool.wait_ge(wh_done, g + 1)
                g_.tensor_tensor(wl[:, :, :, :], wraw[:, :, :, :], wh[:, :, :, :].bitcast(F32),
                                 ALU.subtract).then_inc(w_done, 1)

            with pool.Fori(0, B) as b:
                split_w(b, 0)
                layer_norm(b, 0)

                def pair(p, par):
                    last = isinstance(p, int) and p == PAIRS - 1
                    if not last:
                        split_w(b, p + 1)
                    g = b * PAIRS + p
                    for s in range(STEPS):
                        c, t = divmod(s, TT)
                        if t == 0:
                            pool.wait_ge(sum_full, g * 2 + c - 1 + SUM_CREDIT)
                            continue
                        n = (g * 2 + c) * (TT - 1) + t
                        pool.wait_ge(exp_done, g * STEPS + s + 1 + EXP_CREDIT)
                        if t > 1:
                            pool.wait_ge(presum_done, n - 1 + PRESUM_CREDIT)
                        other = pb[:, (s - 1) % 4, :, :] if t == 1 else acc[:, c, :, :]
                        g_.tensor_tensor(acc[:, c, :, :], other, pb[:, s % 4, :, :],
                                         ALU.add).then_inc(presum_done, 1)

                for_pairs(pool, pair)
                for k in range(1, 4):
                    layer_norm(b, k)

        @block.vector
        def _(dve):
            v = nc.vector
            for s, n in ((exp_done, EXP_CREDIT), (pv_done, PV_CREDIT), (st_full, ST_CREDIT),
                         (presum_done, PRESUM_CREDIT), (sum_full, SUM_CREDIT), (asm_ld, DMA_CREDIT),
                         (m_ld, DMA_CREDIT), (x_st, DMA_CREDIT), (ring_free[0], 1), (ring_free[1], 1),
                         (small_free, 1), (mT_full, 1), (o_free, 1), (norm_done, 1), (y_free, 4),
                         (w_done, 1), (vT_done, 1), (qv_done, 4), (ya_done, 2)):
                dve.sem_inc(s, n)

            dve.wait_ge(silu_done, 1)
            n = 0
            for b in range(B):
                for k in range(KD):
                    v.tensor_copy(scb[:, b, k, :], sc[:, b, k:k + 1].to_broadcast([P, P])).then_inc(scb_done, 1)
            dve.wait_ge(modps, 1)
            for b in range(B):
                v.tensor_tensor(mc[:, :, b], ps[:, 0, 0:32].rearrange("p (j b) -> p j b", b=B)[:, :, b],
                                cols[:, :], ALU.add).then_inc(mod_step, 1)
            dve.wait_ge(modps, 3)
            for b in range(B):
                v.tensor_tensor(gates[:, b, 0:2, :], ps[:, 1 + b, :].rearrange("p (g d) -> p g d", g=2),
                                gb[:, :, :], ALU.add).then_inc(mod_step, 1)
            dve.wait_ge(mod_step, 4)
            for b in range(B):
                v.tensor_scalar(affs[:, b, 0, 0, :], mc[:, 2:4, b], 1.0, None, ALU.add).then_inc(mod_done, 1)
                v.tensor_copy(affs[:, b, 1, 0, :], mc[:, 0:2, b]).then_inc(mod_done, 1)
                v.tensor_scalar(affs[:, b, 0, 1, :], mc[:, 8:10, b], 1.0, None, ALU.add).then_inc(mod_done, 1)
                v.tensor_copy(affs[:, b, 1, 1, :], mc[:, 6:8, b]).then_inc(mod_done, 1)
                v.tensor_copy(affs[:, b, 0, 2, :], lnp[:, 0, :]).then_inc(mod_done, 1)
                v.tensor_copy(affs[:, b, 1, 2, :], lnp[:, 1, :]).then_inc(mod_done, 1)
                v.tensor_scalar(mc[:, 12:14, b], mc[:, 12:14, b], 1.0, None, ALU.add).then_inc(mod_done, 1)
            dve.wait_ge(mod_done, 14)
            for b in range(B):
                v.tensor_tensor(affs[:, b, 0, 3, :], mc[:, 12:14, b], lnp[:, 2, :], ALU.mult).then_inc(mod_done, 1)
                v.tensor_tensor(affs[:, b, 1, 3, :], mc[:, 12:14, b], lnp[:, 3, :], ALU.mult).then_inc(mod_done, 1)
            dve.wait_ge(mod_done, 18)
            for b in range(B):
                v.tensor_tensor(affs[:, b, 1, 3, :], affs[:, b, 1, 3, :], mc[:, 14:16, b], ALU.add).then_inc(mod_done, 1)
            dve.wait_ge(mod_done, 20)

            def statistics(b, k, h, src):
                n = b * 8 + k * 2 + h
                for t in range(h * 4, h * 4 + 4):
                    i = v.bn_stats(stat[:, t, :], src[:, t, :])
                i.then_inc(stat_done, 1)
                wait_alone(dve, stat_done, n + 1, tick)
                for t in range(h * 4, h * 4 + 4):
                    i = v.bn_aggr(mv[:, t, :], stat[:, t, :])
                i.then_inc(mv_done, 1)

            def scale_rows(b, k, h, src):
                n = b * 8 + k * 2 + h
                dve.wait_ge(mv_done, n + 1)
                dve.wait_ge(rstd_done, n + 1)
                for t in range(h * 4, h * 4 + 4):
                    i = v.tensor_scalar(xh[:, t, :], src[:, t, :], mv[:, t, 0:1], rstd[:, t:t + 1],
                                        ALU.subtract, ALU.mult)
                i.then_inc(xhat_done, 1)

            def residual(b, j0, gate, t):
                j = b * 24 + j0 + t
                dve.wait_ge(y_full, j + 1)
                if j0 + t >= 2:
                    dve.wait_ge(resid_done, j - 1)
                v.tensor_tensor(rtmp[:, t % 2, :], y_ps[t % 4], rowbias[:, gate, :], ALU.add).then_inc(y_free, 1)
                dve.wait_ge(y_free, j + 1 + 4)
                v.tensor_tensor(rtmp[:, t % 2, :], rtmp[:, t % 2, :],
                                gates[:, bass.ds(b, 1), gate, :].rearrange("p o d -> p (o d)"),
                                ALU.mult).then_inc(r_step, 1)
                dve.wait_ge(r_step, j + 1)
                v.tensor_tensor(xs[:, t, :], xs[:, t, :], rtmp[:, t % 2, :], ALU.add).then_inc(resid_done, 1)

            def residual_and_norm(b, j0, gate, k):
                for h in range(2):
                    for t in range(h * 4, h * 4 + 4):
                        residual(b, j0, gate, t)
                    dve.wait_ge(resid_done, b * 24 + j0 + 4 * h + 4)
                    statistics(b, k, h, xs)
                    scale_rows(b, k, h, xs)

            def normalise(b, p, c, used):
                g2 = (b * PAIRS + p) * 2 + c
                dve.wait_ge(sum_full, g2 + 1 + SUM_CREDIT)
                dve.wait_ge(norm_done, g2 + 1)
                v.reciprocal(rec[:, :], small_ps).then_inc(small_free, 1)
                dve.wait_ge(small_free, b * SMALL_B + used + 2)
                dve.wait_ge(o_free, g2 + 1 + 1)
                v.tensor_tensor(OT[:, bass.ds(p, 1), c * CH:(c + 1) * CH].rearrange("p o n -> p (o n)"), o_raw[:, :], rec[:, :],
                                ALU.mult).then_inc(norm_done, 1)

            def side(b, p, item, r):
                if item[0] == "proj":
                    k = item[1]
                    bank, before = r.take()
                    if k < 4:
                        dst, lead = (ql, qh) if k % 2 == 0 else (kl, kh)
                        cs = slice((k // 2) * CH, (k // 2 + 1) * CH)
                        dve.wait_ge(lead_done, (b * PAIRS + p) * 4 + k + 1)
                        v.tensor_tensor(dst[:, cs], ring[bank], lead[:, cs].bitcast(F32),
                                        ALU.subtract).then_inc(ring_free[bank], 1)
                        dve.wait_ge(ring_free[bank], before + 2)
                        dve.sem_inc(rest_done, 1)
                elif item[0] == "vt":
                    r.take()
                elif item[0] == "max":
                    taken = []
                    for kc in range(2):
                        bank, before = r.take()
                        taken.append((bank, before))
                        dve.wait_ge(ring_full[bank], before + 1)
                        v.tensor_reduce(mpart[:, item[2], kc:kc + 1], ring[bank], AX.X,
                                        ALU.max).then_inc(ring_free[bank], 1)
                    if item[2] == 7:
                        n = (b * PAIRS + p) * 2 + item[1]
                        for bank, before in taken:
                            dve.wait_ge(ring_free[bank], before + 2)
                        v.tensor_reduce(mx[:, :], mpart[:, :, :], AX.X, ALU.max).then_inc(mx_step, 1)
                        dve.wait_ge(mx_step, 3 * n + 1)
                        dve.wait_ge(mT_full, n + 1)
                        mx_v = mx[:, :].rearrange("p (h t) -> p t h", h=2)
                        v.tensor_copy(ml[:, :, :, 0], mx_v).then_inc(mx_step, 1)
                        dve.wait_ge(mx_step, 3 * n + 2)
                        v.tensor_tensor(ml[:, :, :, 1], mx_v, ml[:, :, :, 0].bitcast(F32),
                                        ALU.subtract).then_inc(mx_step, 1)

            with dve.Fori(0, B) as b:
                v.tensor_copy(aff[:, :, :, :], affs[:, bass.ds(b, 1), :, :, :].rearrange("p o a k j -> p (o a) k j")).then_inc(aff_done, 1)
                dve.wait_ge(x_ld, b * 32 + 32)
                for h in range(2):
                    statistics(b, 0, h, xs)
                for h in range(2):
                    scale_rows(b, 0, h, xs)
                for h in range(2):
                    for k in range(KD):
                        dve.wait_ge(xnh_done, b * 4 + h * 2 + k + 1)
                        cs = slice(h * CH, (h + 1) * CH)
                        v.tensor_tensor(xnl[:, k, cs], xT[:, k, cs], xnh[:, k, cs].bitcast(F32),
                                        ALU.subtract).then_inc(xnl_done, 1)
                for i in range(2):
                    for h in range(2):
                        v.memset(km[i][h][DH:DH + 2, :].bitcast(F32), -1.0).then_inc(neg_done, 1)
                r = Ring(b * (RING_B // 2))
                for item in PROLOGUE:
                    side(b, 0, item, r)

                def pair(p, par):
                    r = Ring(b * (RING_B // 2) + RING_PRO // 2 + p * (RING_IT // 2))
                    for s in range(STEPS):
                        for of_next, *item in side_items(p, s):
                            if item[0] == "sum":
                                if item[1] == 1:
                                    normalise(b, p - 1, 1, small_use(p, ("sum", 1)))
                                else:
                                    normalise(b, p, 0, p * 4 + 2)
                            else:
                                side(b, p + 1 if of_next else p, item, r)

                for_pairs(dve, pair)
                normalise(b, PAIRS - 1, 1, SMALL_B - 1)

                residual_and_norm(b, 0, 0, 1)
                residual_and_norm(b, 8, 1, 2)

                def add_bias(t):
                    dve.wait_ge(qv_full, b * 8 + t + 1)
                    v.tensor_tensor(QV[:, t, :], ps[:, t % 4, :], qvbias[:, :], ALU.add).then_inc(qv_done, 1)

                def heads_of(h):
                    return QV[:, h * 4:h * 4 + 4, 0:D].rearrange("p t (h d) -> p t h d", d=DH1)

                def of_head(x, h):
                    return x[:, h * 4:h * 4 + 4, :].unsqueeze(3).to_broadcast([P, 4, H1, DH1])

                def less_max(h):
                    q = heads_of(h)
                    dve.wait_ge(qv_done, b * 8 + 4 * h + 4 + 4)
                    v.tensor_reduce(qmx[:, h * 4:h * 4 + 4, :], q, AX.X, ALU.max).then_inc(q_step, 1)
                    dve.wait_ge(q_step, b * 6 + 3 * h + 1)
                    v.tensor_tensor(q, q, of_head(qmx, h), ALU.subtract).then_inc(qsub_done, 1)

                def over_sum(h, before):
                    q = heads_of(h)
                    dve.wait_ge(qexp_done, b * 2 + h + 1)
                    v.tensor_reduce(qsum[:, h * 4:h * 4 + 4, :], q, AX.X, ALU.add).then_inc(q_step, 1)
                    dve.wait_ge(q_step, b * 6 + before + 1)
                    v.reciprocal(qrs[:, h * 4:h * 4 + 4, :], qsum[:, h * 4:h * 4 + 4, :]).then_inc(q_step, 1)
                    dve.wait_ge(q_step, b * 6 + before + 2)
                    v.tensor_tensor(q, q, of_head(qrs, h), ALU.mult).then_inc(q_done, 1)

                add_bias(0)
                add_bias(1)
                for h in range(KD):
                    n = b * 6 + h * 3
                    dve.wait_ge(kt_full, b * 2 + h + 1)
                    v.tensor_reduce(kmx[:, h:h + 1], ps[:, 4 + 2 * h:6 + 2 * h, :], AX.XY, ALU.max).then_inc(kb_step, 1)
                    dve.wait_ge(kb_step, n + 1)
                    v.tensor_tensor(ktmp[:, h:h + 1], kmx[:, h:h + 1], bkc[:, h:h + 1], ALU.add).then_inc(kb_step, 1)
                    dve.wait_ge(kb_step, n + 2)
                    v.tensor_tensor(knb[:, h:h + 1], bkc[:, h:h + 1], ktmp[:, h:h + 1], ALU.subtract).then_inc(kb_step, 1)
                add_bias(2)
                add_bias(3)
                less_max(0)
                for t in range(4, TT):
                    add_bias(t)
                over_sum(0, 1)
                less_max(1)
                dve.wait_ge(ke_done, b * 2 + 2)
                v.reciprocal(krs, ksum).then_inc(krs_done, 1)
                over_sum(1, 4)
                dve.wait_ge(krs_done, b + 1)
                for h in range(KD):
                    dve.wait_ge(ctx_full, b * 2 + h + 1)
                    v.scalar_tensor_tensor(cm[:, h, :], ps[:, h, 0:P], krs[:, h:h + 1], blockdiag[:, :],
                                           ALU.mult, ALU.mult).then_inc(ctx_done, 1)
                for h in range(2):
                    dve.wait_ge(ya_done, b * 8 + 4 * h + 4 + 2)
                    statistics(b, 3, h, Y)
                    scale_rows(b, 3, h, Y)
                for t in range(TT):
                    residual(b, 16, 2, t)

        @block.scalar
        def _(act):
            a = nc.scalar
            act.wait_ge(const_ld, 16 * N_CONST_DMAS)
            a.activation(sc[:, :, :], cT[:, :, :], ACT.Silu).then_inc(silu_done, 1)

            def layer_norm(b, k, func, halves=(0, 1)):
                for h in halves:
                    for j in range(KD):
                        n = b * 16 + k * 4 + h * 2 + j
                        act.wait_ge(lnT_full, n + 1)
                        a.activation(xT[:, j, h * CH:(h + 1) * CH], ps[:, 2 * h + j, :], func,
                                     bias=aff[:, 1, k, j:j + 1], scale=aff[:, 0, k, j:j + 1]).then_inc(lnT_done, 1)
                        if k == 0:
                            a.activation(xnh[:, j, h * CH:(h + 1) * CH], ps[:, 2 * h + j, :], func,
                                         bias=aff[:, 1, k, j:j + 1], scale=aff[:, 0, k, j:j + 1]).then_inc(xnh_done, 1)

            def side(b, p, par, item, r, used):
                g = b * PAIRS + p
                if item[0] == "proj":
                    k = item[1]
                    bank, before = r.take()
                    act.wait_ge(ring_full[bank], before + 1)
                    cs = slice((k // 2) * CH, (k // 2 + 1) * CH)
                    if k == 0:
                        act.wait_ge(asm_ld, g * 384 + DMA_CREDIT)
                    if k < 4:
                        lead = qh if k % 2 == 0 else kh
                        a.copy(lead[:, cs], ring[bank]).then_inc(lead_done, 1)
                    else:
                        c = k - 4
                        a.copy(vT[:, c * CH:(c + 1) * CH], ring[bank]).then_inc(vT_done, 1)
                        act.wait_ge(vT_done, 2 * g + c + 1 + 1)
                        act.sem_inc(ring_free[bank], 1)
                elif item[0] == "vt":
                    c = item[1]
                    bank, before = r.take()
                    act.wait_ge(ring_full[bank], before + 1)
                    if c == 0:
                        act.wait_ge(pv_done, g * STEPS + PV_CREDIT - STEPS)
                    a.copy(vn[par][:, c * 4:c * 4 + 4, :],
                           ring[bank].rearrange("p (t n) -> p t n", n=P)).then_inc(ring_free[bank], 1)
                elif item[0] == "max":
                    r.take()
                    r.take()
                elif item[0] == "m":
                    n = g * 2 + item[1]
                    act.wait_ge(mT_full, n + 1 + 1)
                    act.wait_ge(m_ld, 32 * n + DMA_CREDIT)
                    a.copy(mrow[:, :], small_ps[0:4, :]).then_inc(small_free, 1)

            def take_output(b, p, c):
                g = b * PAIRS + p
                act.wait_ge(pv_done, g * STEPS + (c + 1) * TT + PV_CREDIT)
                act.wait_ge(norm_done, g * 2 + c + 1)
                a.copy(o_raw[:, :], o_ps).then_inc(o_free, 1)

            with act.Fori(0, B) as b:
                act.wait_ge(aff_done, b + 1)
                layer_norm(b, 0, ACT.Identity)
                r = Ring(b * (RING_B // 2))
                for item in PROLOGUE:
                    side(b, 0, 0, item, r, 0)

                def pair(p, par):
                    r = Ring(b * (RING_B // 2) + RING_PRO // 2 + p * (RING_IT // 2))
                    g = b * PAIRS + p
                    for s in range(STEPS):
                        S = g * STEPS + s
                        act.wait_ge(st_full, S + 1 + ST_CREDIT)
                        act.wait_ge(pv_done, S - 3 + PV_CREDIT)
                        c, t = divmod(s, TT)
                        done = (g * 2 + c) * (TT - 1) + t - 4 if t > 4 else \
                            (g * 2 + c) * (TT - 1) + 1 if t == 4 else (g * 2 + c - 1) * (TT - 1) + t + 4
                        act.wait_ge(presum_done, done + PRESUM_CREDIT)
                        a.activation(pb[:, s % 4, :, :], st[s % 2], ACT.Exp, scale=DH ** -0.5).then_inc(exp_done, 1)
                        if s == TT:
                            take_output(b, p, 0)
                        for of_next, *item in side_items(p, s):
                            if item[0] != "sum":
                                side(b, p + 1 if of_next else p, 1 - par if of_next else par, item, r, 0)
                    take_output(b, p, 1)

                for_pairs(act, pair)

                for c in range(NC):
                    layer_norm(b, 1, ACT.Identity, [c])
                    for m in range(MB):
                        n = b * 16 + c * MB + m
                        act.wait_ge(h_full, n + 1)
                        a.activation(OT[:, m, c * CH:(c + 1) * CH], ps[:, 4 + m % 4, :], ACT.Gelu,
                                     bias=b1c[:, m:m + 1]).then_inc(gelu_done, 1)
                layer_norm(b, 2, ACT.Identity)
                for h in range(KD):
                    act.wait_ge(kb_step, b * 6 + h * 3 + 3)
                    a.activation(KE[:, h, :], ps[:, 4 + 2 * h:6 + 2 * h, :].rearrange("p c n -> p (c n)"), ACT.Exp,
                                 bias=knb[:, h:h + 1], accum_out=ksum[:, h:h + 1]).then_inc(ke_done, 1)

                def query_exp(h):
                    act.wait_ge(qsub_done, b * 2 + h + 1)
                    a.activation(QV[:, h * 4:h * 4 + 4, 0:D], QV[:, h * 4:h * 4 + 4, 0:D], ACT.Exp).then_inc(qexp_done, 1)

                query_exp(0)
                for h in range(KD):
                    for c in range(2):
                        act.wait_ge(kn_full, b * 4 + h * 2 + c + 1)
                        a.copy(KN[:, c * 4:c * 4 + 4, h * P:(h + 1) * P],
                               ps[:, 4 + 2 * h + c, :].rearrange("p (t n) -> p t n", n=P)).then_inc(kn_done, 1)
                query_exp(1)
                for c in range(2):
                    for h in range(KD):
                        act.wait_ge(qt_full, b * 4 + c * 2 + h + 1)
                        a.copy(QT[:, h, c * CH:(c + 1) * CH], ps[:, 2 + 2 * c + h, :]).then_inc(qt_done, 1)
                for t in range(TT):
                    act.wait_ge(ya_full, b * 8 + t + 1)
                    a.copy(Y[:, t, :], ps[:, 6 + t % 2, 0:D]).then_inc(ya_done, 1)
                layer_norm(b, 3, ACT.Silu)

        @block.tensor
        def _(pe):
            mm = nc.tensor.matmul

            pe.wait_ge(const_ld, 16 * N_CONST_DMAS)
            pe.wait_ge(silu_done, 1)
            for j in range(16):
                w = Wm if j < 12 else We
                col = (j if j < 12 else j - 12) * P
                for k in range(KD):
                    i = mm(ps[:, 0, 2 * j:2 * j + 2], w[:, k, col:col + P], sc[:, :, k], start=(k == 0), stop=(k == KD - 1))
            i.then_inc(modps, 1)
            pe.wait_ge(scb_done, 4)
            for b in range(B):
                for n, first in ((0, 2 * D), (1, 5 * D)):
                    for k in range(KD):
                        i = mm(ps[:, 1 + b, n * D:(n + 1) * D], scb[:, b, k, :], Wm[:, k, first:first + D],
                               start=(k == 0), stop=(k == KD - 1))
                i.then_inc(modps, 1)
            pe.wait_ge(consts, 1)
            pe.wait_ge(wo_ld, 16)

            def layer_norm(b, k, halves=(0, 1)):
                for h in halves:
                    pe.wait_ge(xhat_done, b * 8 + k * 2 + h + 1)
                    for j in range(KD):
                        for t in range(4):
                            i = nc.tensor.transpose(ps[:, 2 * h + j, t * P:(t + 1) * P],
                                                    xh[:, h * 4 + t, j * P:(j + 1) * P], ident[:, :])
                        i.then_inc(lnT_full, 1)

            def side(b, p, par, item, r):
                g = b * PAIRS + p
                if item[0] == "proj":
                    k = item[1]
                    s = k % 2 if k < 4 else 2
                    c = k // 2 if k < 4 else k - 4
                    if k == 0:
                        pe.wait_ge(w_done, g + 1 + 1)
                    bank, before = r.take()
                    pe.wait_ge(ring_free[bank], before + 1)
                    cs = slice(c * CH, (c + 1) * CH)
                    n = 0
                    for kin in range(KD):
                        for w, xx in ((wh, xnh), (wh, xnl), (wl, xnh)):
                            i = mm(ring[bank], w[:, kin, s, :], xx[:, kin, cs], start=(n == 0), stop=(n == 5))
                            n += 1
                    i.then_inc(ring_full[bank], 1)
                elif item[0] == "vt":
                    c = item[1]
                    bank, before = r.take()
                    pe.wait_ge(ring_free[bank], before + 1)
                    pe.wait_ge(vT_done, 2 * g + c + 1 + 1)
                    for t in range(4):
                        n = c * 4 + t
                        i = nc.tensor.transpose(ring[bank][:, t * P:(t + 1) * P], vT[:, n * P:(n + 1) * P], ident[:, :])
                    i.then_inc(ring_full[bank], 1)
                elif item[0] == "max":
                    c, u = item[1], item[2]
                    h, t = divmod(u, TPC)
                    qs = slice(c * CH + t * P, c * CH + (t + 1) * P)
                    if c == 0 and u == 0:
                        pe.wait_ge(asm_ld, (g + 1) * 384 + DMA_CREDIT)
                    for kc in range(2):
                        bank, before = r.take()
                        ks = slice(kc * CH, (kc + 1) * CH)
                        pe.wait_ge(ring_free[bank], before + 1)
                        mm(ring[bank], qq[par][h][:, qs], kk[par][h][:, ks], start=True, stop=False)
                        mm(ring[bank], qm[par][h][0:DH, qs], km[par][h][0:DH, ks], start=False,
                           stop=True).then_inc(ring_full[bank], 1)
                elif item[0] == "m":
                    n = g * 2 + item[1]
                    pe.wait_ge(mx_step, 3 * (n + 1))
                    for t in range(TPC):
                        i = nc.tensor.transpose(small_ps[0:4, t * P:(t + 1) * P],
                                                ml[:, t, :, :].bitcast(F32).rearrange("p h a -> p (h a)"), ident[:, :])
                    i.then_inc(mT_full, 1)

            def row_sums(b, p, c, used):
                g2 = (b * PAIRS + p) * 2 + c
                pe.wait_ge(presum_done, (g2 + 1) * (TT - 1) + PRESUM_CREDIT)
                pe.wait_ge(small_free, b * SMALL_B + used + 1)
                for h in range(2):
                    i = mm(small_ps[h * DH:(h + 1) * DH, :], ones[:, :], acc[:, c, h, :], start=True, stop=True)
                i.then_inc(sum_full, 1)

            def pv(b, p, par, s):
                S = (b * PAIRS + p) * STEPS + s
                c, t = divmod(s, TT)
                pe.wait_ge(exp_done, S + 1 + EXP_CREDIT)
                if t == 0:
                    pe.wait_ge(o_free, (b * PAIRS + p) * 2 + c + 1)
                for h in range(2):
                    hs = slice(h * DH, (h + 1) * DH)
                    i = mm(o_ps[hs, :], vn[par][:, t, hs], pb[:, s % 4, h, :], start=(t == 0), stop=(t == TT - 1))
                i.then_inc(pv_done, 1)

            def product(b, j0, t, lhs, rhs, n):
                j = b * 24 + j0 + t
                pe.wait_ge(y_free, j + 1)
                for k in range(n):
                    i = mm(y_ps[t % 4], lhs[:, k, t * P:(t + 1) * P], rhs[:, k, :], start=(k == 0), stop=(k == n - 1))
                i.then_inc(y_full, 1)

            with pe.Fori(0, B) as b:
                layer_norm(b, 0)
                pe.wait_ge(xnl_done, b * 4 + 2)
                pe.wait_ge(neg_done, b * 4 + 4)
                r = Ring(b * (RING_B // 2))
                for item in PROLOGUE:
                    if item == ("proj", 2):
                        pe.wait_ge(xnl_done, b * 4 + 4)
                    if item[0] == "m":
                        pe.wait_ge(small_free, b * SMALL_B + 1)
                    side(b, 0, 0, item, r)

                def pair(p, par):
                    g = b * PAIRS + p
                    r = Ring(b * (RING_B // 2) + RING_PRO // 2 + p * (RING_IT // 2))
                    for s in range(STEPS):
                        c, t = divmod(s, TT)
                        S = g * STEPS + s
                        if t == 0:
                            pe.wait_ge(m_ld, (g * 2 + c + 1) * 32 + DMA_CREDIT)
                        pe.wait_ge(exp_done, S - 1 + EXP_CREDIT)
                        ks, qs = slice(t * P, (t + 1) * P), slice(c * CH, (c + 1) * CH)
                        for h in range(2):
                            mm(st[s % 2][:, h, :], kk[par][h][:, ks], qq[par][h][:, qs], start=True, stop=False)
                            i = mm(st[s % 2][:, h, :], km[par][h][0:DH + 2, ks], qm[par][h][0:DH + 2, qs],
                                   start=False, stop=True)
                        i.then_inc(st_full, 1)
                        items = side_items(p, s)
                        for n, (of_next, *item) in enumerate(items + [(False, "pv")]):
                            if s > 0 and n == min(1, len(items)):
                                pv(b, p, par, s - 1)
                            if item == ["pv"]:
                                continue
                            if item == ["sum", 1]:
                                row_sums(b, p - 1, 1, small_use(p, ("sum", 1)))
                            elif item == ["sum", 0]:
                                row_sums(b, p, 0, p * 4 + 2)
                            else:
                                if item[0] == "m":
                                    pe.wait_ge(small_free, b * SMALL_B + small_use(p, tuple(item)) + 1)
                                side(b, p + 1 if of_next else p, 1 - par if of_next else par, item, r)
                    pv(b, p, par, STEPS - 1)

                for_pairs(pe, pair)
                row_sums(b, PAIRS - 1, 1, SMALL_B - 1)

                pe.wait_ge(norm_done, (b + 1) * PAIRS * 2 + 1)
                for t in range(TT):
                    product(b, 0, t, OT, Wo, PAIRS)
                pe.wait_ge(post_ld[0], 16 * (b + 1))
                for c in range(NC):
                    layer_norm(b, 1, [c])
                    pe.wait_ge(lnT_done, b * 16 + 4 + 2 * (c + 1))
                    for m in range(MB):
                        n = c * MB + m
                        if n < 4:
                            pe.wait_ge(y_free, b * 24 + 4 + n + 1 + 4)
                        else:
                            pe.wait_ge(gelu_done, b * 16 + n - 3)
                        for k in range(KD):
                            i = mm(ps[:, 4 + m % 4, :], W1s[:, k, m * P:(m + 1) * P], xT[:, k, c * CH:(c + 1) * CH],
                                   start=(k == 0), stop=(k == KD - 1))
                        i.then_inc(h_full, 1)
                pe.wait_ge(post_ld[1], 16 * (b + 1))
                for t in range(TT):
                    if t < 4:
                        pe.wait_ge(gelu_done, b * 16 + 12 + t + 1)
                    product(b, 8, t, OT, W2s, MB)

                def keys(c):
                    for h in range(KD):
                        for k in range(KD):
                            i = mm(ps[:, 4 + 2 * h + c, :], Wks[:, k, h * P:(h + 1) * P], xT[:, k, c * CH:(c + 1) * CH],
                                   start=(k == 0), stop=(k == KD - 1))
                        if c == NC - 1:
                            i.then_inc(kt_full, 1)

                def queries_values(t):
                    pe.wait_ge(qv_done, b * 8 + t + 1)
                    for k in range(KD):
                        i = mm(ps[:, t % 4, :], xT[:, k, t * P:(t + 1) * P], Wqv[:, k, :],
                               start=(k == 0), stop=(k == KD - 1))
                    i.then_inc(qv_full, 1)

                layer_norm(b, 2, [0])
                pe.wait_ge(lnT_done, b * 16 + 8 + 2)
                pe.wait_ge(post_ld[2], 96 * (b + 1))
                queries_values(0)
                queries_values(1)
                pe.wait_ge(y_free, b * 24 + 16 + 4)
                keys(0)
                layer_norm(b, 2, [1])
                pe.wait_ge(lnT_done, b * 16 + 8 + 4)
                keys(1)
                for t in range(2, TT):
                    queries_values(t)
                for h in range(KD):
                    pe.wait_ge(ke_done, b * 2 + h + 1)
                    for c in range(2):
                        for t in range(4):
                            n = c * 4 + t
                            i = nc.tensor.transpose(ps[:, 4 + 2 * h + c, t * P:(t + 1) * P], KE[:, h, n * P:(n + 1) * P], ident[:, :])
                        i.then_inc(kn_full, 1)
                pe.wait_ge(qv_done, b * 8 + 8 + 4)
                for h in range(KD):
                    pe.wait_ge(kn_done, b * 4 + 2 * h + 2)
                    for t in range(TT):
                        i = mm(ps[:, h, 0:P], KN[:, t, h * P:(h + 1) * P], QV[:, t, D + h * P:D + (h + 1) * P],
                               start=(t == 0), stop=(t == TT - 1))
                    i.then_inc(ctx_full, 1)
                for c in range(2):
                    pe.wait_ge(q_done, b * 2 + c + 1)
                    for h in range(KD):
                        for t in range(4):
                            n = c * 4 + t
                            i = nc.tensor.transpose(ps[:, 2 + 2 * c + h, t * P:(t + 1) * P], QV[:, n, h * P:(h + 1) * P], ident[:, :])
                        i.then_inc(qt_full, 1)
                pe.wait_ge(ctx_done, b * 2 + 2)
                for t in range(TT):
                    if t % 4 == 0:
                        pe.wait_ge(qt_done, b * 4 + 2 * (t // 4) + 2)
                    pe.wait_ge(ya_done, b * 8 + t + 1)
                    for h in range(KD):
                        i = mm(ps[:, 6 + t % 2, h * P:(h + 1) * P], QT[:, h, t * P:(t + 1) * P], cm[:, h, :], start=True, stop=True)
                    i.then_inc(ya_full, 1)
                for h in range(2):
                    layer_norm(b, 3, [h])
                    pe.wait_ge(ya_done, b * 8 + 8 + 2)
                    pe.wait_ge(lnT_done, b * 16 + 12 + 2 * (h + 1))
                    for t in range(h * 4, h * 4 + 4):
                        product(b, 16, t, xT, oW, KD)


N_CONST_DMAS = 18

_INS = ['x', 'cond_1024', 'L0_cond_W_mod', 'L0_cond_b_mod', 'L0_cond_W_qkv', 'L0_cond_W_out', 'L0_cond_b_out',
        'L0_cond_W1', 'L0_cond_b1', 'L0_cond_W2', 'L0_cond_b2', 'L1_cond_norm_g', 'L1_cond_norm_b', 'L1_cond_Wq',
        'L1_cond_bq', 'L1_cond_Wk', 'L1_cond_bk', 'L1_cond_Wv', 'L1_cond_bv', 'L1_cond_emb_W', 'L1_cond_emb_b',
        'L1_cond_sn_g', 'L1_cond_sn_b', 'L1_cond_out_W', 'L1_cond_out_b']
_OUTS = [((2, 1024, 256), 'float32')]


def kernel(**inputs):
    import numpy as _np
    import concourse.bacc as _bacc
    from concourse import mybir as _mybir
    from concourse.bass_utils import run_bass_kernel_spmd as _run

    nc = _bacc.Bacc("TRN2", target_bir_lowering=False, num_devices=1)
    arrays, args = {}, []
    for name in _INS:
        a = _np.ascontiguousarray(inputs[name])
        arrays[f"in_{name}_dram"] = a
        args.append(nc.dram_tensor(f"in_{name}_dram", a.shape, _mybir.dt.from_np(a.dtype), kind="ExternalInput").ap())
    for i, (shape, dtype) in enumerate(_OUTS):
        dt = _mybir.dt.from_np(_np.dtype(dtype))
        args.append(nc.dram_tensor(f"out_{i}_dram", shape, dt, kind="ExternalOutput").ap())
    dit_kernel(nc, *args)
    r = _run(nc, [arrays], core_ids=[0])
    got = tuple(r.results[0][f"out_{i}_dram"] for i in range(len(_OUTS)))
    return got[0]
```

```python
from contextlib import ExitStack

import concourse.bass as bass
from concourse import mybir

F32 = mybir.dt.float32
F32R = mybir.dt.float32r
ACT = mybir.ActivationFunctionType
ALU = mybir.AluOpType
AX = mybir.AxisListType

P = 128
B, T, D = 2, 1024, 256
KD = D // P
TT = T // P
CH = 512
NC = T // CH
TPC = CH // P
HEADS, DH = 16, 64
PAIRS = HEADS // 2
MLP = 1024
MB = MLP // P
H1, DH1 = 16, 16
EPS = 1e-5
MOD_OPS = B * 8
STEPS = NC * TT

ST_CREDIT = STEPS + 1
EXP_CREDIT = 2
PV_CREDIT = STEPS + 4
PRESUM_CREDIT = TT - 1
SUM_CREDIT = 2
DMA_CREDIT = 16
Y_CREDIT = 4

RING_PRO = 6 + 2 + 16
RING_IT = 16 + RING_PRO
RING_B = RING_PRO + (PAIRS - 1) * RING_IT + 16
SMALL_B = 4 * PAIRS

BIAS_STEP = 7
LAST_SUM = 9
OT_SPLIT = {0: 0, 1: 1, 2: 2, 3: 3, 4: 4, 5: 5, 10: 6}
WO_SPLIT = 5
LAST_SPLIT = 12
VECTOR_ADDS = 12
NORM_STEP = 10
LN3_BEFORE = 3
LN1_AFTER = 3

SIDE = {
    0: [("max", 1, 0)],
    1: [("max", 1, 1), ("max", 1, 2)],
    2: [("max", 1, 3), ("proj", 0)],
    3: [("proj", 1), ("max", 1, 4)],
    4: [("max", 1, 5), ("max", 1, 6)],
    5: [("max", 1, 7), ("proj", 2)],
    6: [("m", 1), ("proj", 3)],
    7: [("sum", 1), ("proj", 4)],
    8: [("proj", 5)],
    9: [("max", 0, 0), ("max", 0, 1)],
    10: [("max", 0, 2), ("max", 0, 3)],
    11: [("max", 0, 4), ("max", 0, 5)],
    12: [("max", 0, 6), ("max", 0, 7)],
    13: [("m", 0)],
    14: [("vt", 0), ("sum", 0)],
    15: [("vt", 1)],
}
BESIDE_W2 = [("proj", k) for k in (0, 1, 4, 2, 3, 5)] + [("vt", 0), ("vt", 1)]
PROLOGUE = BESIDE_W2 + [("max", 0, u) for u in range(8)] + [("m", 0)]


def small_use(p, item):
    if isinstance(p, int) and (p, item) == (0, ("m", 1)):
        return 1
    if isinstance(p, int) and (p, item) == (PAIRS - 1, ("sum", 0)):
        return p * 4 + 2
    return p * 4 + {("m", 1): 0, ("sum", 1): 1, ("m", 0): 2, ("sum", 0): 3}[item]


def side_items(p, s):
    out = []
    for item in SIDE[s]:
        of_next = item[0] in ("proj", "vt") or item[0] in ("max", "m") and item[1] == 0
        if of_next and isinstance(p, int) and p == PAIRS - 1:
            continue
        if item == ("sum", 1) and isinstance(p, int) and p == 0:
            continue
        if item == ("sum", 0) and isinstance(p, int) and p == PAIRS - 1:
            continue
        out.append((of_next,) + item)
    if s == LAST_SUM and isinstance(p, int) and p == PAIRS - 1:
        out.append((False, "sum", 0))
    return out


def wait_alone(eng, sem, value, tick):
    eng.wait_ge(sem, value)
    eng.sem_inc(tick, 1)


def ln_seq(b, k):
    if k == 0:
        return (b - 1) * 4 + 1 if b else 0
    return b * 4 + k + (1 if b < B - 1 else 0)


class Ring:

    def __init__(self, base):
        self.base, self.k = base, 0

    def take(self):
        bank, before = self.k % 2, self.base + self.k // 2
        self.k += 1
        return bank, before


def for_pairs(eng, emit):
    emit(0, 0)
    with eng.Fori(0, (PAIRS - 2) // 2) as two:
        emit(two * 2 + 1, 1)
        emit(two * 2 + 2, 0)
    emit(PAIRS - 1, 1)


def dit_kernel(nc, x, cond, W_mod, b_mod, W_qkv, W_out, b_out, W1, b1, W2, b2,
               norm_g, norm_b, Wq, bq, Wk, bk, Wv, bv, emb_W, emb_b, sn_g, sn_b, out_W, out_b, out):
    with ExitStack() as ctx:
        place = [(nc.sbuf_base + 31) // 32 * 32]

        def at(name, shape, dt, offset):
            return nc.alloc_sbuf_tensor_at(name, shape, dt, offset=offset)

        def sb(name, shape, dt=F32):
            n = 4
            for s in shape[1:]:
                n *= s
            t = at(name, shape, dt, place[0])
            place[0] += (n + 31) // 32 * 32
            return t

        def sem(name):
            return ctx.enter_context(nc.semaphore(name))

        ident = sb("ident", [P, P])
        ones = sb("ones", [P, DH])
        blockdiag = sb("blockdiag", [P, P])
        gates = sb("gates", [P, B, 3, D])
        rowbias = sb("rowbias", [P, 3, D])
        affs = sb("affs", [P, B, 2, 4, KD])
        gbias = sb("gbias", [P, 1, D])
        b1c = sb("b1c", [P, MB])
        bkc = sb("bkc", [P, KD])
        nhalf = sb("nhalf", [P, TPC])
        small = sb("small", [P, 64])
        ktmp, knb, ksum, krs = small[:, 0:2], small[:, 2:4], small[:, 4:6], small[:, 6:8]
        kmx = small[:, 8:10]
        stat = sb("stat", [P, TT, 6])
        mv = sb("mv", [P, TT, 2])
        veps = sb("veps", [P, TT])
        rstd = sb("rstd", [P, TT])
        xs = sb("xs", [P, TT, D])
        x_next = at("x_next", [P, TT, D], F32, place[0])
        xnh = sb("xnh", [P, KD, T], F32R)
        xn = at("xn", [P, KD, T], F32, place[0])
        xnl = sb("xnl", [P, KD, T], F32R)
        OT0 = place[0]
        OT = sb("OT", [P, PAIRS, T])
        OTl = at("OTl", [P, PAIRS, T], F32R, OT0)
        KE = at("KE", [P, KD, T], F32, OT0)
        KN = at("KN", [P, TT, D], F32, OT0 + 8192)
        QV = at("QV", [P, TT, 2 * D], F32, OT0 + 16384)
        Wo = sb("Wo", [P, PAIRS, D])
        wraw = sb("wraw", [P, KD, 3, P])
        wh = sb("wh", [P, KD, 3, P], F32R)
        wl = sb("wl", [P, KD, 3, P], F32R)
        vn1 = sb("vn1", [P, TT, P])
        xh_next = at("xh_next", [P, TT, D], F32, place[0])
        vn = [sb("vn0", [P, TT, P]), vn1]
        vT = sb("vT", [P, T])
        W2h = at("W2h", [P, MB, D], F32R, place[0])
        acc = sb("acc", [P, NC, 2, CH])
        o_raw = sb("o_raw", [P, CH])
        qvbias = at("qvbias", [P, 2 * D], F32, place[0])
        rec = sb("rec", [P, CH])
        mpart = sb("mpart", [P, 8, 2])
        mx = sb("mx", [P, 8])
        ml = sb("ml", [P, TPC, 2, 2], F32R)
        mrow = sb("mrow", [4, CH], F32R)
        pb0 = place[0]
        pb = sb("pb", [P, 4, 2, CH])
        xh = at("xh", [P, TT, D], F32, pb0)
        xT = at("xT", [P, KD, T], F32, pb0 + 8192)
        xTl = at("xTl", [P, KD, T], F32R, pb0 + 8192)
        Woh = at("Woh", [P, PAIRS, D], F32R, place[0])
        Wof = at("Wof", [P, PAIRS, D], F32, place[0] + 8192)
        Wol = at("Wol", [P, PAIRS, D], F32R, place[0] + 8192)
        parts = sb("parts", [P, 4, T], F32R)
        qh, ql, kh, kl = (parts[:, n, :] for n in range(4))
        k1 = place[0]
        ops = [None, None]
        for par in (1, 0):
            k0 = place[0]
            ops[par] = [sb(f"ops{par}{h}", [P, 4, T], F32R) for h in range(2)]
        qq, kk, qm, km = ([[ops[par][h][:, n, :] for h in range(2)] for par in range(2)] for n in range(4))
        assert place[0] <= nc.sbuf_usable_end, place[0]
        OTh = at("OTh", [P, PAIRS, T], F32R, k0)
        W1s = at("W1s", [P, KD, MLP], F32, k1)
        W1l = at("W1l", [P, KD, MLP], F32R, k1)
        Wqvk = at("Wqvk", [P, KD * 3 * D], F32, k1)
        Wqvkl = at("Wqvkl", [P, KD * 3 * D], F32R, k1)
        oW = at("oW", [P, KD, D], F32, k1 + 6144)
        W2s = at("W2s", [P, MB, D], F32, k1 + 8192)
        W2l = at("W2l", [P, MB, D], F32R, k1 + 8192)
        cm = at("cm", [P, KD, P], F32, k1 + 8192)
        qmx = at("qmx", [P, TT, H1], F32, k1 + 8192 + 1024)
        qsum = at("qsum", [P, TT, H1], F32, k1 + 8192 + 1536)
        qrs = at("qrs", [P, TT, H1], F32, k1 + 8192 + 2048)
        W1h = at("W1h", [P, KD, MLP], F32R, k1 + 16384)
        Wqvkh = at("Wqvkh", [P, KD * 3 * D], F32R, k1 + 16384)
        QT = at("QT", [P, KD, T], F32, k1 + 16384)
        xTh = at("xTh", [P, KD, T], F32R, k1 + 24576)
        Y = at("Y", [P, TT, D], F32, k1 + 24576)

        def qv_of(w):
            return w[:, 0:KD * 2 * D].rearrange("p (k n) -> p k n", k=KD)

        def k_of(w):
            return w[:, KD * 2 * D:KD * 3 * D].rearrange("p (k n) -> p k n", k=KD)

        Wm = at("Wm", [P, KD, 6 * D], F32, k1)
        We = at("We", [P, KD, 2 * D], F32, k1 + 12288)
        cT = at("cT", [P, B, KD], F32, k1 + 16384)
        sc = at("sc", [P, B, KD], F32, k1 + 16384 + 32)
        cols = at("cols", [P, 16], F32, k1 + 16384 + 64)
        mc = at("mc", [P, 16, B], F32, k1 + 16384 + 128)
        lnp = at("lnp", [P, 4, KD], F32, k1 + 16384 + 256)
        gb = at("gb", [P, 2, D], F32, k1 + 16384 + 512)
        scb = at("scb", [P, B, KD, P], F32, k1 + 16384 + 4096)

        ps = ctx.enter_context(nc.psum_tensor("ps", [P, 8, 512], F32))
        st = [ps[:, 0:2, :], ps[:, 2:4, :]]
        o_ps = ps[:, 4, :]
        small_ps = ps[:, 5, :]
        ring = [ps[:, 6, :], ps[:, 7, :]]
        y_ps = [ps[:, n, 0:D] for n in range(4)]

        qv_ps = [ps[:, t if t < 4 else 4 + t % 2, :] for t in range(TT)]

        early_ld, const_ld = sem("early_ld"), sem("const_ld")
        tick = sem("tick")
        wo_ld = sem("wo_ld")
        mask_a, mask_b, consts = sem("mask_a"), sem("mask_b"), sem("consts")
        silu_done, scb_done, msa_ps, msa_step, msa_done = (
            sem("silu_done"), sem("scb_done"), sem("msa_ps"), sem("msa_step"), sem("msa_done"))
        modps, mod_done, mod_step = sem("modps"), sem("mod_done"), sem("mod_step")
        x_ld, xn_ld = [sem("x_ld0"), sem("x_ld1")], [sem("xn_ld0"), sem("xn_ld1")]
        x_st = sem("x_st")
        stat_done, mv_done, veps_done, rstd_done, xhat_done = (
            sem("stat_done"), sem("mv_done"), sem("veps_done"), sem("rstd_done"), sem("xhat_done"))
        lnT_full, lnT_done, xnh_done, xnl_done = sem("lnT_full"), sem("lnT_done"), sem("xnh_done"), sem("xnl_done")
        w_ld, wh_done, w_done, neg_done = sem("w_ld"), sem("wh_done"), sem("w_done"), sem("neg_done")
        ring_full = [sem("ring_full0"), sem("ring_full1")]
        ring_free = [sem("ring_free0"), sem("ring_free1")]
        small_free, mT_full, sum_full = sem("small_free"), sem("mT_full"), sem("sum_full")
        lead_done, rest_done, vT_done = sem("lead_done"), sem("rest_done"), sem("vT_done")
        asm_ld = [sem("asm_ld0"), sem("asm_ld1")]
        mx_step, m_ld = sem("mx_step"), sem("m_ld")
        st_full, exp_done, pv_done, presum_done = sem("st_full"), sem("exp_done"), sem("pv_done"), sem("presum_done")
        o_free, norm_done = sem("o_free"), sem("norm_done")
        y_full, resid_done = sem("y_full"), sem("resid_done")
        gbias_done, bias_done = sem("gbias_done"), sem("bias_done")
        wof_done, w2f_done, ow_done = sem("wof_done"), sem("w2f_done"), sem("ow_done")
        w1_ld, w2_ld, l1_ld = sem("w1_ld"), sem("w2_ld"), sem("l1_ld")
        woh_done, wol_done, w1h_done, w1l_done = sem("woh_done"), sem("wol_done"), sem("w1h_done"), sem("w1l_done")
        w2h_done, w2l_done, l1h_done, l1l_done = sem("w2h_done"), sem("w2l_done"), sem("l1h_done"), sem("l1l_done")
        oh_done, ol_done, xl_done, gl_done = sem("oh_done"), sem("ol_done"), sem("xl_done"), sem("gl_done")
        h_full, gelu_done = sem("h_full"), sem("gelu_done")
        kt_full, kb_step, ke_done, krs_done, kn_full, kn_done = (
            sem("kt_full"), sem("kb_step"), sem("ke_done"), sem("krs_done"), sem("kn_full"), sem("kn_done"))
        qv_full, qv_done, qsub_done, qexp_done, q_step, q_done = (
            sem("qv_full"), sem("qv_done"), sem("qsub_done"), sem("qexp_done"), sem("q_step"), sem("q_done"))
        qt_full, qt_done, ctx_full, ctx_done, ya_full, ya_done = (
            sem("qt_full"), sem("qt_done"), sem("ctx_full"), sem("ctx_done"), sem("ya_full"), sem("ya_done"))

        x_v = x.rearrange("b (t p) d -> b p t d", p=P)
        out_v = out.rearrange("b (t p) d -> b p t d", p=P)
        rows = "(k p) n -> p k n"
        wqkv_v = W_qkv.rearrange("(k p) (s n) -> k p s n", p=P, s=3)

        block = ctx.enter_context(nc.Block())

        @block.sync
        def _(sp):
            sp.dma_start(xs[:, 0:4, :], x_v[0, :, 0:4, :]).then_inc(x_ld[0], 16)
            with nc.allow_non_contiguous_dma(reason="small vectors into columns"):
                for dst, src in ((cT[:, :, :], cond.rearrange("b (k p) -> p b k", p=P)),
                                 (cols[:, 0:12], b_mod.rearrange("(j p) -> p j", p=P)),
                                 (Wm[:, :, 0:2 * D], W_mod.rearrange(rows, p=P)[:, :, 0:2 * D])):
                    sp.dma_start(dst, src).then_inc(early_ld, 16)
            sp.dma_start(xs[:, 4:8, :], x_v[0, :, 4:8, :]).then_inc(x_ld[1], 16)
            def load_w(b, p):
                g = b * PAIRS + p
                sp.wait_ge(w_done, g + 1)
                for k in range(KD):
                    sp.dma_start(wraw[:, k, :, :], wqkv_v[k, :, :, bass.ds(p * P, P)]).then_inc(w_ld, 16)

            def assemble(b, p, par, c):
                g = b * PAIRS + p
                cs = slice(c * CH, (c + 1) * CH)
                if c == 0:
                    sp.wait_ge(st_full, g * STEPS + ST_CREDIT - STEPS)
                sp.wait_ge(rest_done, g * 4 + 2 * c + 2)
                for h in range(2):
                    s = slice(h * DH, (h + 1) * DH)
                    to = ops[par][h]
                    for dst, src in ((to[0:DH, 0:2, cs], parts[s, 0:4:2, cs]),
                                     (to[DH:P, 0:2, cs], parts[s, 1:3, cs]),
                                     (to[0:DH, 2:4, cs], parts[s, 0:4:3, cs])):
                        sp.dma_start(dst.bitcast(F32), src.bitcast(F32)).then_inc(asm_ld[h], 16)

            def max_rows(b, p, par, c, used):
                sp.wait_ge(small_free, b * SMALL_B + used + 2)
                for h in range(2):
                    sp.dma_start(qm[par][h][DH:DH + 2, c * CH:(c + 1) * CH].bitcast(F32),
                                 mrow[2 * h:2 * h + 2, :].bitcast(F32)).then_inc(m_ld, 16)

            load_w(0, 0)
            n = 0
            with nc.allow_non_contiguous_dma(reason="small vectors into columns"):
                for dst, src in [(Wm[:, :, 2 * D:6 * D], W_mod.rearrange(rows, p=P)[:, :, 2 * D:6 * D]),
                                 (We[:, :, :], emb_W.rearrange(rows, p=P)),
                                 (cols[:, 12:16], emb_b.rearrange("(j p) -> p j", p=P)),
                                 (gb[:, 0, :], b_mod[2 * D:3 * D].partition_broadcast(P)),
                                 (gb[:, 1, :], b_mod[5 * D:6 * D].partition_broadcast(P)),
                                 (b1c[:, :], b1.rearrange("(j p) -> p j", p=P)),
                                 (bkc[:, :], bk.rearrange("(j p) -> p j", p=P))] \
                        + [(lnp[:, n, :], v.rearrange("(j p) -> p j", p=P))
                           for n, v in enumerate((norm_g, norm_b, sn_g, sn_b))] \
                        + [(gates[:, b, 2, :], cond[b, :].partition_broadcast(P)) for b in range(B)] \
                        + [(rowbias[:, n, :], v.partition_broadcast(P)) for n, v in enumerate((b_out, b2, out_b))]:
                    sp.dma_start(dst, src).then_inc(const_ld, 16)
                    n += 1
            assert n == N_CONST_DMAS
            load_w(0, 1)
            for c in range(NC):
                assemble(0, 0, 0, c)
            max_rows(0, 0, 0, 0, 0)
            sp.dma_start(Wo[:, :, :], W_out.rearrange(rows, p=P)).then_inc(wo_ld, 16)

            for b in range(B):
                def pair(p, par):
                    last = isinstance(p, int) and p == PAIRS - 1
                    if not last:
                        if not (isinstance(p, int) and p == 0):
                            load_w(b, p + 1)
                        assemble(b, p + 1, 1 - par, 0)
                    elif b < B - 1:
                        load_w(b + 1, 0)
                        sp.wait_ge(vT_done, 2 * (b + 1) * PAIRS + 1)
                        for h in range(2):
                            sp.dma_start(x_next[:, h * 4:h * 4 + 4, :], x_v[b + 1, :, h * 4:h * 4 + 4, :]).then_inc(xn_ld[h], 16)
                    max_rows(b, p, par, 1, small_use(p, ("m", 1)))
                    if not last:
                        assemble(b, p + 1, 1 - par, 1)
                        max_rows(b, p + 1, 1 - par, 0, small_use(p, ("m", 0)))

                for_pairs(sp, pair)
                sp.wait_ge(st_full, (b + 1) * PAIRS * STEPS + ST_CREDIT)
                sp.dma_start(W1s[:, :, :], W1.rearrange(rows, p=P)).then_inc(w1_ld, 16)
                sp.dma_start(W2s[:, :, :], W2.rearrange(rows, p=P)).then_inc(w2_ld, 16)
                sp.wait_ge(norm_done, (b + 1) * PAIRS * 2 + 1)
                sp.dma_start(qvbias[:, 0:D], bq.partition_broadcast(P)).then_inc(l1_ld, 16)
                sp.dma_start(qvbias[:, D:2 * D], bv.partition_broadcast(P)).then_inc(l1_ld, 16)
                sp.wait_ge(h_full, (b + 1) * NC * MB)
                sp.dma_start(qv_of(Wqvk)[:, :, 0:D], Wq.rearrange(rows, p=P)).then_inc(l1_ld, 16)
                sp.dma_start(qv_of(Wqvk)[:, :, D:2 * D], Wv.rearrange(rows, p=P)).then_inc(l1_ld, 16)
                sp.dma_start(k_of(Wqvk), Wk.rearrange(rows, p=P)).then_inc(l1_ld, 16)
                sp.dma_start(oW[:, :, :], out_W.rearrange(rows, p=P)).then_inc(l1_ld, 16)
                if b < B - 1:
                    load_w(b + 1, 1)
                    sp.wait_ge(y_full, b * 24 + 16)
                    for c in range(NC):
                        assemble(b + 1, 0, 0, c)
                    max_rows(b + 1, 0, 0, 0, 0)
                for h in range(2):
                    sp.wait_ge(resid_done, b * 24 + 16 + 4 * (h + 1) + Y_CREDIT)
                    sp.dma_start(out_v[b, :, h * 4:h * 4 + 4, :], xs[:, h * 4:h * 4 + 4, :]).then_inc(x_st, 16)
                sp.wait_ge(x_st, (b + 1) * 32)
                if b < B - 1:
                    for h in range(2):
                        sp.dma_start(xs[:, h * 4:h * 4 + 4, :], x_v[b + 1, :, h * 4:h * 4 + 4, :]).then_inc(x_ld[h], 16)

        @block.gpsimd
        def _(pool):
            g_ = nc.gpsimd
            g_.memset(ident[:, :], 0.0).then_inc(mask_a, 1)
            g_.memset(blockdiag[:, :], 1.0).then_inc(mask_a, 1)
            g_.memset(ones[:, :], 1.0).then_inc(mask_a, 1)
            g_.memset(nhalf[:, :], -0.5).then_inc(mask_a, 1)
            pool.wait_ge(mask_a, 4)
            g_.affine_select(out=ident[:, :], in_=ident[:, :], compare_op=ALU.not_equal, fill=1.0, base=0,
                             pattern=[[-1, P]], channel_multiplier=1).then_inc(mask_b, 1)
            bd = blockdiag[:, :].rearrange("p (c l) -> p c l", l=DH1)
            g_.affine_select(out=bd, in_=bd, compare_op=ALU.is_ge, fill=0.0, base=0,
                             pattern=[[-DH1, P // DH1], [0, DH1]], channel_multiplier=1).then_inc(mask_b, 1)
            pool.wait_ge(mask_b, 2)
            g_.affine_select(out=bd, in_=bd, compare_op=ALU.is_ge, fill=0.0, base=DH1 - 1,
                             pattern=[[DH1, P // DH1], [0, DH1]], channel_multiplier=-1).then_inc(consts, 1)

            def minus_ones(par, before):
                for h in range(2):
                    g_.memset(km[par][h][DH:DH + 2, :].bitcast(F32), -1.0).then_inc(neg_done, 1)
                    pool.wait_ge(neg_done, before + h + 1)

            def layer_norm(b, k, halves=(0, 1)):
                for h in halves:
                    n = ln_seq(b, k) * 2 + h
                    hs = slice(h * 4, h * 4 + 4)
                    pool.wait_ge(mv_done, n + 1)
                    g_.tensor_scalar(veps[:, hs], mv[:, hs, 1], EPS, 1.0, ALU.add, ALU.mult).then_inc(veps_done, 1)
                    pool.wait_ge(veps_done, n + 1)
                    g_.tensor_tensor(rstd[:, hs], veps[:, hs], nhalf[:, :], ALU.pow).then_inc(rstd_done, 1)

            def split_w(b, p):
                g = b * PAIRS + p
                pool.wait_ge(w_ld, 32 * (g + 1))
                wait_alone(pool, vT_done, 2 * g + 1, tick)
                g_.tensor_copy(wh[:, :, :, :], wraw[:, :, :, :]).then_inc(wh_done, 1)
                pool.wait_ge(wh_done, g + 1)
                g_.tensor_tensor(wl[:, :, :, :], wraw[:, :, :, :], wh[:, :, :, :].bitcast(F32),
                                 ALU.subtract).then_inc(w_done, 1)

            pool.wait_ge(consts, 1)
            minus_ones(0, 0)
            layer_norm(0, 0)
            split_w(0, 0)
            split_w(0, 1)
            for b in range(B):
                def pair(p, par):
                    if not (isinstance(p, int) and p in (0, PAIRS - 1)):
                        split_w(b, p + 1)
                    elif p == PAIRS - 1 and b < B - 1:
                        split_w(b + 1, 0)
                    g = b * PAIRS + p
                    for s in range(STEPS):
                        c, t = divmod(s, TT)
                        last = isinstance(p, int) and p == PAIRS - 1
                        if last and b < B - 1 and s == NORM_STEP:
                            pool.wait_ge(presum_done, (g * 2 + 1) * (TT - 1) + min(s, VECTOR_ADDS) - 1 - TT + PRESUM_CREDIT)
                            layer_norm(b + 1, 0, [0])
                        if last and s >= VECTOR_ADDS:
                            continue
                        if t == 0:
                            pool.wait_ge(sum_full, g * 2 + c - 1 + SUM_CREDIT)
                            continue
                        n = (g * 2 + c) * (TT - 1) + t
                        pool.wait_ge(exp_done, g * STEPS + s + 1 + EXP_CREDIT)
                        if isinstance(p, int) and p == 0 and s == 1:
                            pool.wait_ge(w_done, g + 1 + 1 + 1)
                            minus_ones(1, 2 + 4 * b)
                        if t > 1:
                            pool.wait_ge(presum_done, n - 1 + PRESUM_CREDIT)
                        other = pb[:, (s - 1) % 4, :, :] if t == 1 else acc[:, c, :, :]
                        g_.tensor_tensor(acc[:, c, :, :], other, pb[:, s % 4, :, :],
                                         ALU.add).then_inc(presum_done, 1)

                for_pairs(pool, pair)
                another = b < B - 1
                def add_bias(k):
                    pool.wait_ge(xhat_done, (ln_seq(b, k) + 1) * 2)
                    g_.tensor_tensor(gbias[:, :, :], gates[:, b, k:k + 1, :], rowbias[:, k:k + 1, :],
                                     ALU.mult).then_inc(gbias_done, 1)
                    pool.wait_ge(gbias_done, 3 * b + k + 1)
                    g_.tensor_tensor(xs[:, :, :], xs[:, :, :], gbias[:, :, :].to_broadcast([P, TT, D]),
                                     ALU.add).then_inc(bias_done, 1)
                    pool.wait_ge(bias_done, 3 * b + k + 1)

                if another:
                    layer_norm(b + 1, 0, [1])
                pool.wait_ge(w1h_done, b + 1)
                g_.tensor_tensor(W1l[:, :, :], W1s[:, :, :], W1h[:, :, :].bitcast(F32), ALU.subtract).then_inc(w1l_done, 1)
                pool.wait_ge(w1l_done, b + 1)
                layer_norm(b, 1, [0])
                pool.wait_ge(w2_ld, 16 * (b + 1))
                g_.tensor_tensor(W2s[:, :, :], W2s[:, :, :], gates[:, b, 1:2, :].to_broadcast([P, MB, D]),
                                 ALU.mult).then_inc(w2f_done, 1)
                pool.wait_ge(w2f_done, b + 1)
                layer_norm(b, 1, [1])
                pool.wait_ge(w2h_done, b + 1)
                g_.tensor_tensor(W2l[:, :, :], W2s[:, :, :], W2h[:, :, :].bitcast(F32), ALU.subtract).then_inc(w2l_done, 1)
                pool.wait_ge(w2l_done, b + 1)
                add_bias(1)
                pool.wait_ge(l1h_done, b + 1)
                g_.tensor_tensor(Wqvkl[:, :], Wqvk[:, :], Wqvkh[:, :].bitcast(F32), ALU.subtract).then_inc(l1l_done, 1)
                pool.wait_ge(l1l_done, b + 1)
                g_.tensor_tensor(oW[:, :, :], oW[:, :, :], gates[:, b, 2:3, :].to_broadcast([P, KD, D]),
                                 ALU.mult).then_inc(ow_done, 1)
                pool.wait_ge(ow_done, b + 1)
                layer_norm(b, 2)
                add_bias(2)
                if another:
                    pool.wait_ge(y_full, b * 24 + 16)
                    pool.wait_ge(rstd_done, (ln_seq(b, 2) + 1) * 2)
                    minus_ones(0, 4 + 4 * b)
                    split_w(b + 1, 1)
                layer_norm(b, 3)

        @block.vector
        def _(dve):
            v = nc.vector
            for s, n in ((exp_done, EXP_CREDIT), (pv_done, PV_CREDIT), (st_full, ST_CREDIT),
                         (presum_done, PRESUM_CREDIT), (sum_full, SUM_CREDIT), (asm_ld[0], DMA_CREDIT), (asm_ld[1], DMA_CREDIT),
                         (m_ld, DMA_CREDIT), (ring_free[0], 1), (ring_free[1], 1),
                         (small_free, 1), (mT_full, 1), (o_free, 1), (norm_done, 1), (resid_done, Y_CREDIT),
                         (w_done, 1), (vT_done, 1), (qv_done, 4), (ya_done, 2)):
                dve.sem_inc(s, n)

            def first_modulation():
                dve.wait_ge(msa_ps, 1)
                for b in range(B):
                    v.tensor_tensor(mc[:, 0:4, b], ps[:, 0, 0:8].rearrange("p (j b) -> p j b", b=B)[:, :, b],
                                    cols[:, 0:4], ALU.add).then_inc(msa_step, 1)
                dve.wait_ge(msa_step, 2)
                for b in range(B):
                    v.tensor_scalar(affs[:, b, 0, 0, :], mc[:, 2:4, b], 1.0, None, ALU.add).then_inc(msa_done, 1)
                    v.tensor_copy(affs[:, b, 1, 0, :], mc[:, 0:2, b]).then_inc(msa_done, 1)

            def modulation():
                dve.wait_ge(modps, 3)
                for b in range(B):
                    v.tensor_tensor(mc[:, 6:10, b], ps[:, 4, 0:8].rearrange("p (j b) -> p j b", b=B)[:, :, b],
                                    cols[:, 6:10], ALU.add).then_inc(mod_step, 1)
                    v.tensor_tensor(mc[:, 12:16, b], ps[:, 4, 8:16].rearrange("p (j b) -> p j b", b=B)[:, :, b],
                                    cols[:, 12:16], ALU.add).then_inc(mod_step, 1)
                for b in range(B):
                    v.tensor_tensor(gates[:, b, 0:2, :], ps[:, 2 + b, :].rearrange("p (g d) -> p g d", g=2),
                                    gb[:, :, :], ALU.add).then_inc(mod_step, 1)
                dve.wait_ge(mod_step, 6)
                for b in range(B):
                    v.tensor_scalar(affs[:, b, 0, 1, :], mc[:, 8:10, b], 1.0, None, ALU.add).then_inc(mod_done, 1)
                    v.tensor_copy(affs[:, b, 1, 1, :], mc[:, 6:8, b]).then_inc(mod_done, 1)
                    v.tensor_copy(affs[:, b, 0, 2, :], lnp[:, 0, :]).then_inc(mod_done, 1)
                    v.tensor_copy(affs[:, b, 1, 2, :], lnp[:, 1, :]).then_inc(mod_done, 1)
                    v.tensor_scalar(mc[:, 12:14, b], mc[:, 12:14, b], 1.0, None, ALU.add).then_inc(mod_done, 1)
                dve.wait_ge(mod_done, 10)
                for b in range(B):
                    v.tensor_tensor(affs[:, b, 0, 3, :], mc[:, 12:14, b], lnp[:, 2, :], ALU.mult).then_inc(mod_done, 1)
                    v.tensor_tensor(affs[:, b, 1, 3, :], mc[:, 12:14, b], lnp[:, 3, :], ALU.mult).then_inc(mod_done, 1)
                dve.wait_ge(mod_done, 14)
                for b in range(B):
                    v.tensor_tensor(affs[:, b, 1, 3, :], affs[:, b, 1, 3, :], mc[:, 14:16, b], ALU.add).then_inc(mod_done, 1)
                dve.wait_ge(mod_done, MOD_OPS)

            def tile_statistics(src, t):
                i = v.bn_stats(stat[:, t, :], src[:, t, :])
                if t % 4 == 3:
                    i.then_inc(stat_done, 1)

            def statistics(b, k, h, src=None):
                n = ln_seq(b, k) * 2 + h
                if src is not None:
                    for t in range(h * 4, h * 4 + 4):
                        tile_statistics(src, t)
                dve.wait_ge(stat_done, n + 1)
                for t in range(h * 4, h * 4 + 4):
                    i = v.bn_aggr(mv[:, t, :], stat[:, t, :])
                i.then_inc(mv_done, 1)

            def scale_rows(b, k, h, src):
                n = ln_seq(b, k) * 2 + h
                to = xh_next if k == 0 else xh
                dve.wait_ge(mv_done, n + 1)
                dve.wait_ge(rstd_done, n + 1)
                for t in range(h * 4, h * 4 + 4):
                    i = v.tensor_scalar(to[:, t, :], src[:, t, :], mv[:, t, 0:1], rstd[:, t:t + 1],
                                        ALU.subtract, ALU.mult)
                i.then_inc(xhat_done, 1)

            def residual(b, j0, t):
                j = b * 24 + j0 + t
                dve.wait_ge(y_full, j + 1)
                v.tensor_tensor(xs[:, t, :], xs[:, t, :], y_ps[t % 4], ALU.add).then_inc(resid_done, 1)

            def normalise(b, p, c, used):
                g2 = (b * PAIRS + p) * 2 + c
                dve.wait_ge(sum_full, g2 + 1 + SUM_CREDIT)
                dve.wait_ge(norm_done, g2 + 1)
                v.reciprocal(rec[:, :], small_ps).then_inc(small_free, 1)
                dve.wait_ge(small_free, b * SMALL_B + used + 2)
                dve.wait_ge(o_free, g2 + 1 + 1)
                v.tensor_tensor(OT[:, bass.ds(p, 1), c * CH:(c + 1) * CH].rearrange("p o n -> p (o n)"), o_raw[:, :], rec[:, :],
                                ALU.mult).then_inc(norm_done, 1)

            def side(b, p, item, r):
                if item[0] == "proj":
                    k = item[1]
                    bank, before = r.take()
                    if k < 4:
                        dst, lead = (ql, qh) if k % 2 == 0 else (kl, kh)
                        cs = slice((k // 2) * CH, (k // 2 + 1) * CH)
                        dve.wait_ge(lead_done, (b * PAIRS + p) * 4 + k + 1)
                        v.tensor_tensor(dst[:, cs], ring[bank], lead[:, cs].bitcast(F32),
                                        ALU.subtract).then_inc(ring_free[bank], 1)
                        dve.wait_ge(ring_free[bank], before + 2)
                        dve.sem_inc(rest_done, 1)
                elif item[0] == "vt":
                    r.take()
                elif item[0] == "max":
                    taken = []
                    for kc in range(2):
                        bank, before = r.take()
                        taken.append((bank, before))
                        dve.wait_ge(ring_full[bank], before + 1)
                        v.tensor_reduce(mpart[:, item[2], kc:kc + 1], ring[bank], AX.X,
                                        ALU.max).then_inc(ring_free[bank], 1)
                    if item[2] == 7:
                        n = (b * PAIRS + p) * 2 + item[1]
                        for bank, before in taken:
                            dve.wait_ge(ring_free[bank], before + 2)
                        v.tensor_reduce(mx[:, :], mpart[:, :, :], AX.X, ALU.max).then_inc(mx_step, 1)
                        dve.wait_ge(mx_step, 3 * n + 1)
                        dve.wait_ge(mT_full, n + 1)
                        mx_v = mx[:, :].rearrange("p (h t) -> p t h", h=2)
                        v.tensor_copy(ml[:, :, :, 0], mx_v).then_inc(mx_step, 1)
                        dve.wait_ge(mx_step, 3 * n + 2)
                        v.tensor_tensor(ml[:, :, :, 1], mx_v, ml[:, :, :, 0].bitcast(F32),
                                        ALU.subtract).then_inc(mx_step, 1)

            def norm_rest(b, h):
                for k in range(KD):
                    dve.wait_ge(lnT_done, (ln_seq(b, 0) * 2 + h) * 2 + k + 1)
                    cs = slice(h * CH, (h + 1) * CH)
                    v.tensor_tensor(xnl[:, k, cs], xn[:, k, cs], xnh[:, k, cs].bitcast(F32),
                                    ALU.subtract).then_inc(xnl_done, 1)

            def attention_rest(b, p, cs):
                dve.wait_ge(oh_done, b * (PAIRS + 1) + p + (2 if p == PAIRS - 1 and cs.start else 1))
                v.tensor_tensor(OTl[:, p, cs], OT[:, p, cs], OTh[:, p, cs].bitcast(F32), ALU.subtract).then_inc(ol_done, 1)

            def gelu_rest(b, n):
                c, m = divmod(n, MB)
                cs = slice(c * CH, (c + 1) * CH)
                dve.wait_ge(gelu_done, b * 16 + n + 1)
                v.tensor_tensor(OTl[:, m, cs], OT[:, m, cs], OTh[:, m, cs].bitcast(F32), ALU.subtract).then_inc(gl_done, 1)

            def rows_rest(b, k, h):
                for j in range(KD):
                    dve.wait_ge(lnT_done, (ln_seq(b, k) * 2 + h) * 2 + j + 1)
                    cs = slice(h * CH, (h + 1) * CH)
                    v.tensor_tensor(xTl[:, j, cs], xT[:, j, cs], xTh[:, j, cs].bitcast(F32), ALU.subtract).then_inc(xl_done, 1)

            for h in range(2):
                dve.wait_ge(x_ld[h], 16)
                statistics(0, 0, h, xs)
            for h in range(2):
                scale_rows(0, 0, h, xs)
            first_modulation()
            for h in range(2):
                norm_rest(0, h)
            dve.wait_ge(silu_done, 1)
            for b in range(B):
                for k in range(KD):
                    v.tensor_copy(scb[:, b, k, :], sc[:, b, k:k + 1].to_broadcast([P, P])).then_inc(scb_done, 1)
            r = Ring(0)
            for item in PROLOGUE:
                side(0, 0, item, r)
            modulation()

            for b in range(B):
                next_ring = Ring((b + 1) * (RING_B // 2))

                def beside(*wanted):
                    for item in wanted:
                        if b < B - 1:
                            side(b + 1, 0, item, next_ring)

                def first_norm_of_next(h):
                    if b < B - 1:
                        dve.wait_ge(xn_ld[h], (b + 1) * 16)
                        statistics(b + 1, 0, h, x_next)
                        scale_rows(b + 1, 0, h, x_next)

                def pair(p, par):
                    r = Ring(b * (RING_B // 2) + RING_PRO // 2 + p * (RING_IT // 2))
                    for s in range(STEPS):
                        if s >= VECTOR_ADDS and isinstance(p, int) and p == PAIRS - 1:
                            g = b * PAIRS + p
                            n = (g * 2 + 1) * (TT - 1) + s - TT
                            dve.wait_ge(exp_done, g * STEPS + s + 1 + EXP_CREDIT)
                            dve.wait_ge(presum_done, n - 1 + PRESUM_CREDIT)
                            v.tensor_tensor(acc[:, 1, :, :], acc[:, 1, :, :], pb[:, s % 4, :, :], ALU.add).then_inc(presum_done, 1)
                        for of_next, *item in side_items(p, s):
                            if item[0] == "sum":
                                if item[1] == 1:
                                    normalise(b, p - 1, 1, small_use(p, ("sum", 1)))
                                else:
                                    normalise(b, p, 0, small_use(p, ("sum", 0)))
                            else:
                                side(b, p + 1 if of_next else p, item, r)
                        if isinstance(p, int) and p == 0 and s == BIAS_STEP:
                            v.tensor_tensor(gbias[:, :, :], gates[:, b, 0:1, :], rowbias[:, 0:1, :], ALU.mult).then_inc(gbias_done, 1)
                            for h in range(2):
                                dve.wait_ge(x_ld[h], (b + 1) * 16)
                            dve.wait_ge(gbias_done, 3 * b + 1)
                            v.tensor_tensor(xs[:, :, :], xs[:, :, :], gbias[:, :, :].to_broadcast([P, TT, D]),
                                            ALU.add).then_inc(bias_done, 1)
                        if isinstance(p, int) and p == PAIRS - 1:
                            if s == NORM_STEP:
                                first_norm_of_next(0)
                            if s == LAST_SPLIT:
                                attention_rest(b, PAIRS - 1, slice(0, CH))
                            if s in OT_SPLIT:
                                attention_rest(b, OT_SPLIT[s], slice(0, T))
                            if s == WO_SPLIT - 1:
                                for h in range(2):
                                    dve.wait_ge(asm_ld[h], (b + 1) * PAIRS * 96 + DMA_CREDIT)
                                dve.wait_ge(wo_ld, 16)
                                v.tensor_tensor(Wof[:, :, :], Wo[:, :, :], gates[:, b, 0:1, :].to_broadcast([P, PAIRS, D]),
                                                ALU.mult).then_inc(wof_done, 1)
                            if s == WO_SPLIT:
                                dve.wait_ge(woh_done, b + 1)
                                v.tensor_tensor(Wol[:, :, :], Wof[:, :, :], Woh[:, :, :].bitcast(F32),
                                                ALU.subtract).then_inc(wol_done, 1)

                for_pairs(dve, pair)
                normalise(b, PAIRS - 1, 1, SMALL_B - 1)
                attention_rest(b, PAIRS - 1, slice(CH, T))
                dve.wait_ge(norm_done, (b + 1) * PAIRS * 2 + 1)

                dve.wait_ge(bias_done, 3 * b + 1)
                for h in range(2):
                    for t in range(h * 4, h * 4 + 4):
                        if t == 6:
                            rows_rest(b, 1, 0)
                        residual(b, 0, t)
                        dve.wait_ge(resid_done, b * 24 + t + 1 + Y_CREDIT)
                        tile_statistics(xs, t)
                        if t == 1:
                            first_norm_of_next(1)
                    statistics(b, 1, h)
                    scale_rows(b, 1, h, xs)
                if b < B - 1:
                    for h in range(2):
                        norm_rest(b + 1, h)
                for n in range(NC * MB):
                    gelu_rest(b, n)
                    if n == LN1_AFTER:
                        rows_rest(b, 1, 1)
                dve.wait_ge(l1_ld, 96 * b + 96)
                dve.wait_ge(bias_done, 3 * b + 2)
                for h in range(2):
                    for t in range(h * 4, h * 4 + 4):
                        if t == 7:
                            rows_rest(b, 2, 0)
                        residual(b, 8, t)
                        dve.wait_ge(resid_done, b * 24 + 8 + t + 1 + Y_CREDIT)
                        tile_statistics(xs, t)
                        beside(BESIDE_W2[t])
                    statistics(b, 2, h)
                    scale_rows(b, 2, h, xs)

                def add_bias(t):
                    dve.wait_ge(qv_full, b * 8 + t + 1)
                    v.tensor_tensor(QV[:, t, :], qv_ps[t], qvbias[:, :], ALU.add).then_inc(qv_done, 1)

                def heads_of(h):
                    return QV[:, h * 4:h * 4 + 4, 0:D].rearrange("p t (h d) -> p t h d", d=DH1)

                def of_head(x, h):
                    return x[:, h * 4:h * 4 + 4, :].unsqueeze(3).to_broadcast([P, 4, H1, DH1])

                def less_max(h):
                    q = heads_of(h)
                    dve.wait_ge(qv_done, b * 8 + 4 * h + 4 + 4)
                    v.tensor_reduce(qmx[:, h * 4:h * 4 + 4, :], q, AX.X, ALU.max).then_inc(q_step, 1)
                    dve.wait_ge(q_step, b * 6 + 3 * h + 1)
                    v.tensor_tensor(q, q, of_head(qmx, h), ALU.subtract).then_inc(qsub_done, 1)

                def over_sum(h, before):
                    q = heads_of(h)
                    dve.wait_ge(qexp_done, b * 2 + h + 1)
                    v.tensor_reduce(qsum[:, h * 4:h * 4 + 4, :], q, AX.X, ALU.add).then_inc(q_step, 1)
                    dve.wait_ge(q_step, b * 6 + before + 1)
                    v.reciprocal(qrs[:, h * 4:h * 4 + 4, :], qsum[:, h * 4:h * 4 + 4, :]).then_inc(q_step, 1)
                    dve.wait_ge(q_step, b * 6 + before + 2)
                    v.tensor_tensor(q, q, of_head(qrs, h), ALU.mult).then_inc(q_done, 1)

                add_bias(0)
                add_bias(1)
                add_bias(2)
                add_bias(3)
                rows_rest(b, 2, 1)
                less_max(0)
                for t in range(4, TT):
                    add_bias(t)
                over_sum(0, 1)
                for h in range(KD):
                    n = b * 6 + h * 3
                    dve.wait_ge(kt_full, b * 2 + h + 1)
                    v.tensor_reduce(kmx[:, h:h + 1], ps[:, 2 * h:2 * h + 2, :], AX.XY, ALU.max).then_inc(kb_step, 1)
                    dve.wait_ge(kb_step, n + 1)
                    v.tensor_tensor(ktmp[:, h:h + 1], kmx[:, h:h + 1], bkc[:, h:h + 1], ALU.add).then_inc(kb_step, 1)
                    dve.wait_ge(kb_step, n + 2)
                    v.tensor_tensor(knb[:, h:h + 1], bkc[:, h:h + 1], ktmp[:, h:h + 1], ALU.subtract).then_inc(kb_step, 1)
                less_max(1)
                beside(("max", 0, 0), ("max", 0, 1), ("max", 0, 2))
                dve.wait_ge(ke_done, b * 2 + 2)
                v.reciprocal(krs, ksum).then_inc(krs_done, 1)
                over_sum(1, 4)
                dve.wait_ge(krs_done, b + 1)
                for h in range(KD):
                    dve.wait_ge(ctx_full, b * 2 + h + 1)
                    v.scalar_tensor_tensor(cm[:, h, :], ps[:, h, 0:P], krs[:, h:h + 1], blockdiag[:, :],
                                           ALU.mult, ALU.mult).then_inc(ctx_done, 1)
                beside(("max", 0, 3), ("max", 0, 4), ("max", 0, 5))
                for h in range(2):
                    for t in range(4 * h, 4 * h + 4):
                        dve.wait_ge(ya_done, b * 8 + t + 1 + 2)
                        tile_statistics(Y, t)
                    statistics(b, 3, h)
                    scale_rows(b, 3, h, Y)
                    beside(("max", 0, 6 + h))
                dve.wait_ge(bias_done, 3 * b + 3)
                for t in range(TT):
                    residual(b, 16, t)

        @block.scalar
        def _(act):
            a = nc.scalar
            act.wait_ge(early_ld, 48)
            a.activation(sc[:, :, :], cT[:, :, :], ACT.Silu).then_inc(silu_done, 1)

            def layer_norm(b, k, func, halves=(0, 1)):
                for h in halves:
                    for j in range(KD):
                        n = (ln_seq(b, k) * 2 + h) * 2 + j
                        cs = slice(h * CH, (h + 1) * CH)
                        act.wait_ge(lnT_full, n + 1)
                        if k == 0:
                            lead = xnh
                        elif k < 3:
                            lead = xTh
                        if k < 3:
                            a.activation(lead[:, j, cs], ps[:, 4 + j, :], func,
                                         bias=affs[:, b, 1, k, j:j + 1], scale=affs[:, b, 0, k, j:j + 1])
                        to = xn[:, j, cs] if k == 0 else xT[:, j, cs]
                        a.activation(to, ps[:, 4 + j, :], func,
                                     bias=affs[:, b, 1, k, j:j + 1], scale=affs[:, b, 0, k, j:j + 1]).then_inc(lnT_done, 1)

            def side(b, p, par, item, r):
                g = b * PAIRS + p
                if item[0] == "proj":
                    k = item[1]
                    bank, before = r.take()
                    act.wait_ge(ring_full[bank], before + 1)
                    cs = slice((k // 2) * CH, (k // 2 + 1) * CH)
                    if k == 0:
                        for h in range(2):
                            act.wait_ge(asm_ld[h], g * 96 + DMA_CREDIT)
                    if k < 4:
                        lead = qh if k % 2 == 0 else kh
                        a.copy(lead[:, cs], ring[bank]).then_inc(lead_done, 1)
                    else:
                        c = k - 4
                        a.copy(vT[:, c * CH:(c + 1) * CH], ring[bank]).then_inc(vT_done, 1)
                        act.wait_ge(vT_done, 2 * g + c + 1 + 1)
                        act.sem_inc(ring_free[bank], 1)
                elif item[0] == "vt":
                    c = item[1]
                    bank, before = r.take()
                    act.wait_ge(ring_full[bank], before + 1)
                    if c == 0:
                        act.wait_ge(pv_done, g * STEPS + PV_CREDIT - STEPS)
                    a.copy(vn[par][:, c * 4:c * 4 + 4, :],
                           ring[bank].rearrange("p (t n) -> p t n", n=P)).then_inc(ring_free[bank], 1)
                elif item[0] == "max":
                    r.take()
                    r.take()
                elif item[0] == "m":
                    n = g * 2 + item[1]
                    act.wait_ge(mT_full, n + 1 + 1)
                    act.wait_ge(m_ld, 32 * n + DMA_CREDIT)
                    a.copy(mrow[:, :], small_ps[0:4, :]).then_inc(small_free, 1)

            def attention_lead(b, p, cs):
                last_half = p == PAIRS - 1 and cs.stop == CH
                act.wait_ge(norm_done, (b * PAIRS + p) * 2 + (1 if last_half else 2) + 1)
                a.copy(OTh[:, p, cs], OT[:, p, cs]).then_inc(oh_done, 1)

            def take_output(b, p, c):
                g = b * PAIRS + p
                act.wait_ge(pv_done, g * STEPS + (c + 1) * TT + PV_CREDIT)
                act.wait_ge(norm_done, g * 2 + c + 1)
                a.copy(o_raw[:, :], o_ps).then_inc(o_free, 1)

            act.wait_ge(msa_done, 4)
            layer_norm(0, 0, ACT.Identity)
            r = Ring(0)
            for item in PROLOGUE:
                side(0, 0, 0, item, r)
            act.wait_ge(mod_done, MOD_OPS)
            for b in range(B):
                next_ring = Ring((b + 1) * (RING_B // 2))

                def beside(*wanted):
                    for item in wanted:
                        if b < B - 1:
                            side(b + 1, 0, 0, item, next_ring)

                def pair(p, par):
                    r = Ring(b * (RING_B // 2) + RING_PRO // 2 + p * (RING_IT // 2))
                    g = b * PAIRS + p
                    for s in range(STEPS):
                        S = g * STEPS + s
                        act.wait_ge(st_full, S + 1 + ST_CREDIT)
                        act.wait_ge(pv_done, S - 3 + PV_CREDIT)
                        c, t = divmod(s, TT)
                        done = (g * 2 + c) * (TT - 1) + t - 4 if t > 4 else \
                            (g * 2 + c) * (TT - 1) + 1 if t == 4 else (g * 2 + c - 1) * (TT - 1) + t + 4
                        act.wait_ge(presum_done, done + PRESUM_CREDIT)
                        a.activation(pb[:, s % 4, :, :], st[s % 2], ACT.Exp, scale=DH ** -0.5).then_inc(exp_done, 1)
                        if s == 0 and not (isinstance(p, int) and p == 0):
                            take_output(b, p - 1, 1)
                        if s == TT:
                            take_output(b, p, 0)
                        for of_next, *item in side_items(p, s):
                            if item[0] != "sum":
                                side(b, p + 1 if of_next else p, 1 - par if of_next else par, item, r)
                        if isinstance(p, int) and p == PAIRS - 1:
                            if s == LAST_SPLIT:
                                attention_lead(b, PAIRS - 1, slice(0, CH))
                            if s in OT_SPLIT:
                                attention_lead(b, OT_SPLIT[s], slice(0, T))
                            if s == WO_SPLIT:
                                act.wait_ge(wof_done, b + 1)
                                a.copy(Woh[:, :, :], Wof[:, :, :]).then_inc(woh_done, 1)

                for_pairs(act, pair)
                take_output(b, PAIRS - 1, 1)
                attention_lead(b, PAIRS - 1, slice(CH, T))
                act.wait_ge(w1_ld, 16 * (b + 1))
                a.copy(W1h[:, :, :], W1s[:, :, :]).then_inc(w1h_done, 1)

                if b < B - 1:
                    act.wait_ge(xhat_done, (ln_seq(b + 1, 0) + 1) * 2)
                    layer_norm(b + 1, 0, ACT.Identity)
                layer_norm(b, 1, ACT.Identity, [0])
                act.wait_ge(w2f_done, b + 1)
                a.copy(W2h[:, :, :], W2s[:, :, :]).then_inc(w2h_done, 1)
                for n in range(NC * MB):
                    c, m = divmod(n, MB)
                    act.wait_ge(h_full, b * 16 + n + 1)
                    cs = slice(c * CH, (c + 1) * CH)
                    a.activation(OTh[:, m, cs], ps[:, m % 4, :], ACT.Gelu, bias=b1c[:, m:m + 1])
                    a.activation(OT[:, m, cs], ps[:, m % 4, :], ACT.Gelu,
                                 bias=b1c[:, m:m + 1]).then_inc(gelu_done, 1)
                    if n == LN1_AFTER:
                        layer_norm(b, 1, ACT.Identity, [1])
                act.wait_ge(l1_ld, 96 * (b + 1))
                a.copy(Wqvkh[:, :], Wqvk[:, :]).then_inc(l1h_done, 1)
                beside(*BESIDE_W2[:7])
                layer_norm(b, 2, ACT.Identity, [0])
                beside(BESIDE_W2[7])
                layer_norm(b, 2, ACT.Identity, [1])

                def query_exp(h):
                    act.wait_ge(qsub_done, b * 2 + h + 1)
                    a.activation(QV[:, h * 4:h * 4 + 4, 0:D], QV[:, h * 4:h * 4 + 4, 0:D], ACT.Exp).then_inc(qexp_done, 1)

                query_exp(0)
                for h in range(KD):
                    act.wait_ge(kb_step, b * 6 + h * 3 + 3)
                    a.activation(KE[:, h, :], ps[:, 2 * h:2 * h + 2, :].rearrange("p c n -> p (c n)"), ACT.Exp,
                                 bias=knb[:, h:h + 1], accum_out=ksum[:, h:h + 1]).then_inc(ke_done, 1)
                query_exp(1)
                for h in range(KD):
                    for c in range(2):
                        act.wait_ge(kn_full, b * 4 + h * 2 + c + 1)
                        a.copy(KN[:, c * 4:c * 4 + 4, h * P:(h + 1) * P],
                               ps[:, 2 * h + c, :].rearrange("p (t n) -> p t n", n=P)).then_inc(kn_done, 1)
                for c in range(2):
                    for h in range(KD):
                        act.wait_ge(qt_full, b * 4 + c * 2 + h + 1)
                        a.copy(QT[:, h, c * CH:(c + 1) * CH], ps[:, 4 + h, :]).then_inc(qt_done, 1)
                for t in range(TT):
                    act.wait_ge(ya_full, b * 8 + t + 1)
                    a.copy(Y[:, t, :], ps[:, 2 + t % 2, 0:D]).then_inc(ya_done, 1)
                layer_norm(b, 3, ACT.Silu)
                beside(*[("max", 0, u) for u in range(8)], ("m", 0))

        @block.tensor
        def _(pe):
            mm = nc.tensor.matmul

            def modulation_column(bank, n, j):
                w = Wm if j < 12 else We
                col = (j if j < 12 else j - 12) * P
                for k in range(KD):
                    i = mm(ps[:, bank, 2 * n:2 * n + 2], w[:, k, col:col + P], sc[:, :, k], start=(k == 0), stop=(k == KD - 1))
                return i

            def gates_eighth(u):
                b, n, k = u // 4, u // 2 % 2, u % 2
                first = (2 * D, 5 * D)[n]
                i = mm(ps[:, 2 + b, n * D:(n + 1) * D], scb[:, b, k, :], Wm[:, k, first:first + D],
                       start=(k == 0), stop=(k == KD - 1))
                if u % 4 == 3:
                    i.then_inc(modps, 1)

            def layer_norm(b, k, h):
                n = ln_seq(b, k) * 2 + h
                pe.wait_ge(xhat_done, n + 1)
                if n:
                    pe.wait_ge(lnT_done, 2 * n)
                rows_of = xh_next if k == 0 else xh
                for j in range(KD):
                    for t in range(4):
                        i = nc.tensor.transpose(ps[:, 4 + j, t * P:(t + 1) * P],
                                                rows_of[:, h * 4 + t, j * P:(j + 1) * P], ident[:, :])
                    i.then_inc(lnT_full, 1)

            def side(b, p, par, item, r):
                g = b * PAIRS + p
                if item[0] == "proj":
                    k = item[1]
                    s = k % 2 if k < 4 else 2
                    c = k // 2 if k < 4 else k - 4
                    if k == 0:
                        pe.wait_ge(w_done, g + 1 + 1)
                    bank, before = r.take()
                    pe.wait_ge(ring_free[bank], before + 1)
                    cs = slice(c * CH, (c + 1) * CH)
                    n = 0
                    for kin in range(KD):
                        for w, xx in ((wh, xnh), (wh, xnl), (wl, xnh)):
                            i = mm(ring[bank], w[:, kin, s, :], xx[:, kin, cs], start=(n == 0), stop=(n == 5))
                            n += 1
                    i.then_inc(ring_full[bank], 1)
                elif item[0] == "vt":
                    c = item[1]
                    bank, before = r.take()
                    pe.wait_ge(ring_free[bank], before + 1)
                    pe.wait_ge(vT_done, 2 * g + c + 1 + 1)
                    for t in range(4):
                        n = c * 4 + t
                        i = nc.tensor.transpose(ring[bank][:, t * P:(t + 1) * P], vT[:, n * P:(n + 1) * P], ident[:, :])
                    i.then_inc(ring_full[bank], 1)
                elif item[0] == "max":
                    c, u = item[1], item[2]
                    h, t = divmod(u, TPC)
                    qs = slice(c * CH + t * P, c * CH + (t + 1) * P)
                    if c == 0 and t == 0:
                        pe.wait_ge(asm_ld[h], (g + 1) * 96 + DMA_CREDIT)
                    for kc in range(2):
                        bank, before = r.take()
                        ks = slice(kc * CH, (kc + 1) * CH)
                        pe.wait_ge(ring_free[bank], before + 1)
                        mm(ring[bank], qq[par][h][:, qs], kk[par][h][:, ks], start=True, stop=False)
                        mm(ring[bank], qm[par][h][0:DH, qs], km[par][h][0:DH, ks], start=False,
                           stop=True).then_inc(ring_full[bank], 1)
                elif item[0] == "m":
                    n = g * 2 + item[1]
                    pe.wait_ge(mx_step, 3 * (n + 1))
                    for t in range(TPC):
                        i = nc.tensor.transpose(small_ps[0:4, t * P:(t + 1) * P],
                                                ml[:, t, :, :].bitcast(F32).rearrange("p h a -> p (h a)"), ident[:, :])
                    i.then_inc(mT_full, 1)

            def row_sums(b, p, c, used):
                g2 = (b * PAIRS + p) * 2 + c
                pe.wait_ge(presum_done, (g2 + 1) * (TT - 1) + PRESUM_CREDIT)
                pe.wait_ge(small_free, b * SMALL_B + used + 1)
                for h in range(2):
                    i = mm(small_ps[h * DH:(h + 1) * DH, :], ones[:, :], acc[:, c, h, :], start=True, stop=True)
                i.then_inc(sum_full, 1)

            def pv(b, p, par, s):
                S = (b * PAIRS + p) * STEPS + s
                c, t = divmod(s, TT)
                pe.wait_ge(exp_done, S + 1 + EXP_CREDIT)
                if t == 0:
                    pe.wait_ge(o_free, (b * PAIRS + p) * 2 + c + 1)
                for h in range(2):
                    hs = slice(h * DH, (h + 1) * DH)
                    i = mm(o_ps[hs, :], vn[par][:, t, hs], pb[:, s % 4, h, :], start=(t == 0), stop=(t == TT - 1))
                i.then_inc(pv_done, 1)

            def product(b, j0, t, terms, n, ready=None):
                j = b * 24 + j0 + t
                pe.wait_ge(resid_done, j + 1)
                for k in range(n):
                    if k == n - 1 and ready is not None:
                        pe.wait_ge(ol_done, ready)
                    for lhs, rhs in terms:
                        i = mm(y_ps[t % 4], lhs[:, k, t * P:(t + 1) * P], rhs[:, k, :],
                               start=(k == 0 and lhs is terms[0][0] and rhs is terms[0][1]),
                               stop=(k == n - 1 and lhs is terms[-1][0]))
                i.then_inc(y_full, 1)

            def of_parts(xh_, xl_, wh_, wl_):
                return ((xh_, wh_), (xh_, wl_), (xl_, wh_))

            pe.wait_ge(consts, 1)
            pe.wait_ge(early_ld, 48)
            pe.wait_ge(silu_done, 1)
            for j in range(4):
                i = modulation_column(0, j, j)
            i.then_inc(msa_ps, 1)
            layer_norm(0, 0, 0)
            layer_norm(0, 0, 1)
            r = Ring(0)
            for item in PROLOGUE:
                if item == ("proj", 0):
                    pe.wait_ge(xnl_done, 2)
                if item == ("proj", 2):
                    pe.wait_ge(xnl_done, 4)
                if item == ("max", 0, 0):
                    pe.wait_ge(lnT_done, 4)
                    pe.wait_ge(scb_done, 4)
                    pe.wait_ge(const_ld, 16 * N_CONST_DMAS)
                if item[0] == "m":
                    pe.wait_ge(small_free, 1)
                side(0, 0, 0, item, r)
                if item[0] == "max":
                    gates_eighth(item[2])
            for n, j in enumerate((6, 7, 8, 9, 12, 13, 14, 15)):
                i = modulation_column(4, n, j)
            i.then_inc(modps, 1)
            for b in range(B):
                next_ring = Ring((b + 1) * (RING_B // 2))

                def beside(*wanted):
                    for item in wanted:
                        if b < B - 1:
                            side(b + 1, 0, 0, item, next_ring)

                def pair(p, par):
                    g = b * PAIRS + p
                    r = Ring(b * (RING_B // 2) + RING_PRO // 2 + p * (RING_IT // 2))
                    for s in range(STEPS):
                        c, t = divmod(s, TT)
                        S = g * STEPS + s
                        if isinstance(p, int) and p == 0 and s == 1:
                            if b == 0:
                                pe.wait_ge(mod_step, 6)
                            else:
                                pe.wait_ge(resid_done, b * 24 + 4)
                        if t == 0:
                            pe.wait_ge(m_ld, (g * 2 + c + 1) * 32 + DMA_CREDIT)
                        pe.wait_ge(exp_done, S - 1 + EXP_CREDIT)
                        ks, qs = slice(t * P, (t + 1) * P), slice(c * CH, (c + 1) * CH)
                        for h in range(2):
                            mm(st[s % 2][:, h, :], kk[par][h][:, ks], qq[par][h][:, qs], start=True, stop=False)
                            i = mm(st[s % 2][:, h, :], km[par][h][0:DH + 2, ks], qm[par][h][0:DH + 2, qs],
                                   start=False, stop=True)
                        i.then_inc(st_full, 1)
                        items = side_items(p, s)
                        for n, (of_next, *item) in enumerate(items + [(False, "pv")]):
                            if n == (0 if items and items[0][1] == "m" else min(1, len(items))):
                                if s > 0:
                                    pv(b, p, par, s - 1)
                                elif not isinstance(p, int) or p > 0:
                                    pv(b, p - 1, 1 - par, STEPS - 1)
                            if item == ["pv"]:
                                continue
                            if item == ["sum", 1]:
                                row_sums(b, p - 1, 1, small_use(p, ("sum", 1)))
                            elif item == ["sum", 0]:
                                row_sums(b, p, 0, small_use(p, ("sum", 0)))
                            else:
                                if item[0] == "m":
                                    pe.wait_ge(small_free, b * SMALL_B + small_use(p, tuple(item)) + 1)
                                side(b, p + 1 if of_next else p, 1 - par if of_next else par, item, r)
                    if isinstance(p, int) and p == 0:
                        pe.wait_ge(neg_done, 4 + 4 * b)

                for_pairs(pe, pair)
                pv(b, PAIRS - 1, 1, STEPS - 1)
                pe.wait_ge(wol_done, b + 1)
                for t in range(TT):
                    if t == 0:
                        pe.wait_ge(ol_done, (b + 1) * (PAIRS + 1) - 1)
                    product(b, 0, t, of_parts(OTh, OTl, Woh, Wol), PAIRS,
                            (b + 1) * (PAIRS + 1) if t == TPC else None)
                    if t == 0:
                        row_sums(b, PAIRS - 1, 1, SMALL_B - 1)
                    if t == 2:
                        pe.wait_ge(o_free, (b + 1) * PAIRS * 2 + 1)
                        pe.wait_ge(small_free, (b + 1) * SMALL_B + 1)
                    if b < B - 1 and t in (2, 5):
                        layer_norm(b + 1, 0, t // 4)
                    if t == 6:
                        layer_norm(b, 1, 0)
                pe.wait_ge(w1l_done, b + 1)
                for c in range(NC):
                    pe.wait_ge(xl_done, b * 8 + 2 * c + 2)
                    for m in range(MB):
                        n = c * MB + m
                        if n < 4:
                            pe.wait_ge(resid_done, b * 24 + 4 + n + 1 + 4)
                        else:
                            pe.wait_ge(gelu_done, b * 16 + n - 3)
                        for k in range(KD):
                            for x, w in of_parts(xTh, xTl, W1h, W1l):
                                i = mm(ps[:, m % 4, :], w[:, k, m * P:(m + 1) * P], x[:, k, c * CH:(c + 1) * CH],
                                       start=(k == 0 and w is W1h and x is xTh), stop=(k == KD - 1 and x is xTl))
                        i.then_inc(h_full, 1)
                        if n == LN1_AFTER:
                            layer_norm(b, 1, 1)
                pe.wait_ge(w2l_done, b + 1)
                if b < B - 1:
                    pe.wait_ge(xnl_done, (b + 1) * 4 + 4)
                for t in range(TT):
                    if t < 4:
                        pe.wait_ge(gelu_done, b * 16 + 12 + t + 1)
                    if t % TPC == 0:
                        pe.wait_ge(gl_done, b * 16 + 8 + 8 * (t // TPC))
                    product(b, 8, t, of_parts(OTh, OTl, W2h, W2l), MB)
                    beside(BESIDE_W2[t])
                    if t == 6:
                        layer_norm(b, 2, 0)

                def keys(c):
                    for h in range(KD):
                        for k in range(KD):
                            for x, w in of_parts(xTh, xTl, Wqvkh, Wqvkl):
                                i = mm(ps[:, 2 * h + c, :], k_of(w)[:, k, h * P:(h + 1) * P], x[:, k, c * CH:(c + 1) * CH],
                                       start=(k == 0 and w is Wqvkh and x is xTh), stop=(k == KD - 1 and x is xTl))
                        if c == NC - 1:
                            i.then_inc(kt_full, 1)

                def queries_values(t):
                    if t < 4:
                        pe.wait_ge(resid_done, b * 24 + 12 + t + 1 + 4)
                    elif t >= 6:
                        pe.wait_ge(qv_done, b * 8 + t - 2 + 1 + 4)
                    for k in range(KD):
                        for x, w in of_parts(xTh, xTl, Wqvkh, Wqvkl):
                            i = mm(qv_ps[t], x[:, k, t * P:(t + 1) * P], qv_of(w)[:, k, :],
                                   start=(k == 0 and w is Wqvkh and x is xTh), stop=(k == KD - 1 and x is xTl))
                    i.then_inc(qv_full, 1)

                def queries_transposed(c):
                    for h in range(KD):
                        for t in range(4):
                            n = c * 4 + t
                            i = nc.tensor.transpose(ps[:, 4 + h, t * P:(t + 1) * P], QV[:, n, h * P:(h + 1) * P], ident[:, :])
                        i.then_inc(qt_full, 1)

                pe.wait_ge(xl_done, b * 8 + 4 + 2)
                pe.wait_ge(l1l_done, b + 1)
                queries_values(0)
                queries_values(1)
                queries_values(2)
                queries_values(3)
                layer_norm(b, 2, 1)
                pe.wait_ge(qv_done, b * 8 + 3 + 4)
                keys(0)
                pe.wait_ge(xl_done, b * 8 + 4 + 4)
                for t in range(4, TT):
                    queries_values(t)
                pe.wait_ge(qv_done, b * 8 + 4 + 4)
                keys(1)
                beside(("max", 0, 0))
                pe.wait_ge(qv_done, b * 8 + 8 + 4)
                pe.wait_ge(q_done, b * 2 + 1)
                queries_transposed(0)
                for h in range(KD):
                    pe.wait_ge(ke_done, b * 2 + h + 1)
                    for c in range(2):
                        for t in range(4):
                            n = c * 4 + t
                            i = nc.tensor.transpose(ps[:, 2 * h + c, t * P:(t + 1) * P], KE[:, h, n * P:(n + 1) * P], ident[:, :])
                        i.then_inc(kn_full, 1)
                beside(("max", 0, 1), ("max", 0, 2))
                for h in range(KD):
                    pe.wait_ge(kn_done, b * 4 + 2 * h + 2)
                    for t in range(TT):
                        i = mm(ps[:, h, 0:P], KN[:, t, h * P:(h + 1) * P], QV[:, t, D + h * P:D + (h + 1) * P],
                               start=(t == 0), stop=(t == TT - 1))
                    i.then_inc(ctx_full, 1)
                pe.wait_ge(q_done, b * 2 + 2)
                pe.wait_ge(qt_done, b * 4 + 2)
                queries_transposed(1)
                beside(("max", 0, 3), ("max", 0, 4), ("max", 0, 5))
                pe.wait_ge(ctx_done, b * 2 + 2)
                for t in range(TT):
                    if t % 4 == 0:
                        pe.wait_ge(qt_done, b * 4 + 2 * (t // 4) + 2)
                    pe.wait_ge(ya_done, b * 8 + t + 1)
                    for h in range(KD):
                        i = mm(ps[:, 2 + t % 2, h * P:(h + 1) * P], QT[:, h, t * P:(t + 1) * P], cm[:, h, :], start=True, stop=True)
                    i.then_inc(ya_full, 1)
                beside(("max", 0, 6))
                pe.wait_ge(ya_done, b * 8 + 8 + 2)
                pe.wait_ge(ow_done, b + 1)
                layer_norm(b, 3, 0)
                beside(("max", 0, 7))
                pe.wait_ge(lnT_done, ln_seq(b, 3) * 4 + 2)
                for t in range(TT):
                    if t == LN3_BEFORE:
                        layer_norm(b, 3, 1)
                    if t == TPC:
                        pe.wait_ge(lnT_done, ln_seq(b, 3) * 4 + 4)
                        if b < B - 1:
                            pe.wait_ge(small_free, (b + 1) * SMALL_B + 1)
                            beside(("m", 0))
                    product(b, 16, t, ((xT, oW),), KD)
                if b < B - 1:
                    pe.wait_ge(neg_done, 6 + 4 * b)
                pe.wait_ge(resid_done, (b + 1) * 24 + 4 - 2)


N_CONST_DMAS = 16

_INS = ['x', 'cond_1024', 'L0_cond_W_mod', 'L0_cond_b_mod', 'L0_cond_W_qkv', 'L0_cond_W_out', 'L0_cond_b_out',
        'L0_cond_W1', 'L0_cond_b1', 'L0_cond_W2', 'L0_cond_b2', 'L1_cond_norm_g', 'L1_cond_norm_b', 'L1_cond_Wq',
        'L1_cond_bq', 'L1_cond_Wk', 'L1_cond_bk', 'L1_cond_Wv', 'L1_cond_bv', 'L1_cond_emb_W', 'L1_cond_emb_b',
        'L1_cond_sn_g', 'L1_cond_sn_b', 'L1_cond_out_W', 'L1_cond_out_b']
_OUTS = [((2, 1024, 256), 'float32')]


def kernel(**inputs):
    import numpy as _np
    import concourse.bacc as _bacc
    from concourse import mybir as _mybir
    from concourse.bass_utils import run_bass_kernel_spmd as _run

    nc = _bacc.Bacc("TRN2", target_bir_lowering=False, num_devices=1)
    arrays, args = {}, []
    for name in _INS:
        a = _np.ascontiguousarray(inputs[name])
        arrays[f"in_{name}_dram"] = a
        args.append(nc.dram_tensor(f"in_{name}_dram", a.shape, _mybir.dt.from_np(a.dtype), kind="ExternalInput").ap())
    for i, (shape, dtype) in enumerate(_OUTS):
        dt = _mybir.dt.from_np(_np.dtype(dtype))
        args.append(nc.dram_tensor(f"out_{i}_dram", shape, dt, kind="ExternalOutput").ap())
    dit_kernel(nc, *args)
    r = _run(nc, [arrays], core_ids=[0])
    got = tuple(r.results[0][f"out_{i}_dram"] for i in range(len(_OUTS)))
    return got[0]
```
